# Optimizing a Trainium2 kernel written in Bass

```python
import numpy as np
import jax
import jax.numpy as jnp

def _softmax(x, axis=-1):
    return jax.nn.softmax(x, axis=axis)

def _gelu(x):
    return jax.nn.gelu(x, approximate=True)

def _silu(x):
    return jax.nn.silu(x)

def _sigmoid(x):
    return jax.nn.sigmoid(x)

def _layernorm(x, axis=-1, eps=1e-05):
    m = jnp.mean(x, axis=axis, keepdims=True)
    v = jnp.var(x, axis=axis, keepdims=True)
    return (x - m) / jnp.sqrt(v + eps)

def _scatter_add(tgt, idx, src, axis=0):
    return tgt.at[idx].add(src)

def _segment_sum(src, seg, n):
    return jax.ops.segment_sum(src, seg, n)
kernel_name = 'mk_macaron_d1_jaxref_r8_aae1bf'

def setup_inputs(seed: int=0):
    np.random.seed(seed)
    _w = jnp.asarray

    def _L0_attn_setup():
        import jax, jax.numpy as jnp
        import numpy as np
        B, S, D = (2, 256, 256)
        H, DH, GROUPS = (16, 128, 4)
        KV = H // GROUPS
        G = GROUPS
        key = jax.random.key(seed)
        ks = jax.random.split(key, 5)
        sd = 1.0 / np.sqrt(D)
        return {'x': jax.random.normal(ks[0], (B, S, D), dtype=jnp.float32), 'Wq': jax.random.normal(ks[1], (D, H * DH), dtype=jnp.float32) * sd, 'bq': jnp.zeros((H * DH,), dtype=jnp.float32), 'Wk': jax.random.normal(ks[2], (D, KV * DH), dtype=jnp.float32) * sd, 'bk': jnp.zeros((KV * DH,), dtype=jnp.float32), 'Wv': jax.random.normal(ks[3], (D, KV * DH), dtype=jnp.float32) * sd, 'bv': jnp.zeros((KV * DH,), dtype=jnp.float32), 'Wo': jax.random.normal(ks[4], (H * DH, D), dtype=jnp.float32) * (1.0 / np.sqrt(H * DH)), 'bo': jnp.zeros((D,), dtype=jnp.float32)}
    _L0_attn_in = _L0_attn_setup()

    def _L0_ffn_setup():
        import jax, jax.numpy as jnp
        import numpy as np
        B, S, D = (1, 128, 256)
        E, K, F = (64, 8, 96)
        C = 32

        def _moe(x, router_w, w1, v1, w2):
            T = x.shape[0]
            logits = x @ router_w.T
            probs = jax.nn.softmax(logits, axis=-1)
            wts, idx = jax.lax.top_k(probs, K)
            wts = wts / jnp.sum(wts, axis=-1, keepdims=True)
            R = T * K
            e_flat = idx.reshape(-1)
            tok = jnp.arange(R) // K
            order = jnp.argsort(e_flat)
            e_s, tok_s = (e_flat[order], tok[order])
            w_s = wts.reshape(-1)[order]
            counts = jnp.bincount(e_flat, length=E)
            starts = jnp.cumsum(counts) - counts
            pos = jnp.arange(R) - starts[e_s]
            valid = pos < C
            pos_c = jnp.minimum(pos, C - 1)
            xg = jnp.zeros((E, C, D), x.dtype).at[e_s, pos_c].add(jnp.where(valid[:, None], x[tok_s], 0.0))
            h = jax.nn.silu(jnp.einsum('ecd,efd->ecf', xg, w1)) * jnp.einsum('ecd,efd->ecf', xg, v1)
            y = jnp.einsum('ecf,efd->ecd', h, w2)
            yr = y[e_s, pos_c] * jnp.where(valid, w_s, 0.0)[:, None]
            return jnp.zeros((T, D), x.dtype).at[tok_s].add(yr)
        key = jax.random.key(seed)
        k0, k1, k2, k3, k4 = jax.random.split(key, 5)
        return {'hidden_states': jax.random.normal(k0, (B, S, D), jnp.float32), 'router_w': jax.random.normal(k1, (E, D), jnp.float32) * 0.02, 'w1': jax.random.normal(k2, (E, F, D), jnp.float32) * 0.02, 'v1': jax.random.normal(k3, (E, F, D), jnp.float32) * 0.02, 'w2': jax.random.normal(k4, (E, F, D), jnp.float32) * 0.02}
    _L0_ffn_in = _L0_ffn_setup()
    _d = {'L0_attn_x': _L0_attn_in['x'], 'L0_attn_Wq': _L0_attn_in['Wq'], 'L0_attn_bq': _L0_attn_in['bq'], 'L0_attn_Wk': _L0_attn_in['Wk'], 'L0_attn_bk': _L0_attn_in['bk'], 'L0_attn_Wv': _L0_attn_in['Wv'], 'L0_attn_bv': _L0_attn_in['bv'], 'L0_attn_Wo': _L0_attn_in['Wo'], 'L0_attn_bo': _L0_attn_in['bo'], 'L0_ffn_router_w': _L0_ffn_in['router_w'], 'L0_ffn_w1': _L0_ffn_in['w1'], 'L0_ffn_v1': _L0_ffn_in['v1'], 'L0_ffn_w2': _L0_ffn_in['w2']}
    _x0 = _d['L0_attn_x']
    _d['L0_attn_x'] = jax.random.normal(jax.random.fold_in(jax.random.key(seed), 1), (8, 256, 256), dtype=_x0.dtype)
    del _x0
    return _d

def reference(L0_attn_x, L0_attn_Wq, L0_attn_bq, L0_attn_Wk, L0_attn_bk, L0_attn_Wv, L0_attn_bv, L0_attn_Wo, L0_attn_bo, L0_ffn_router_w, L0_ffn_w1, L0_ffn_v1, L0_ffn_w2):

    def _L0_attn_ref(x, Wq, bq, Wk, bk, Wv, bv, Wo, bo):
        import jax, jax.numpy as jnp
        import numpy as np
        B, S, D = (2, 256, 256)
        H, DH, GROUPS = (16, 128, 4)
        KV = H // GROUPS
        G = GROUPS
        b, s, _ = x.shape
        Q = (x @ Wq + bq).reshape(b, s, KV, G, DH)
        K = (x @ Wk + bk).reshape(b, s, KV, DH)
        V = (x @ Wv + bv).reshape(b, s, KV, DH)
        scale = 1.0 / np.sqrt(DH).astype(np.float32)
        scores = jnp.einsum('bqkgd,bpkd->bkgqp', Q, K) * scale
        attn = jax.nn.softmax(scores, axis=-1)
        out = jnp.einsum('bkgqp,bpkd->bqkgd', attn, V)
        out = out.reshape(b, s, H * DH)
        return out @ Wo + bo

    def _L0_ffn_ref(hidden_states, router_w, w1, v1, w2):
        import jax, jax.numpy as jnp
        import numpy as np
        B, S, D = (1, 128, 256)
        E, K, F = (64, 8, 96)
        C = 32

        def _moe(x, router_w, w1, v1, w2):
            T = x.shape[0]
            logits = x @ router_w.T
            probs = jax.nn.softmax(logits, axis=-1)
            wts, idx = jax.lax.top_k(probs, K)
            wts = wts / jnp.sum(wts, axis=-1, keepdims=True)
            R = T * K
            e_flat = idx.reshape(-1)
            tok = jnp.arange(R) // K
            order = jnp.argsort(e_flat)
            e_s, tok_s = (e_flat[order], tok[order])
            w_s = wts.reshape(-1)[order]
            counts = jnp.bincount(e_flat, length=E)
            starts = jnp.cumsum(counts) - counts
            pos = jnp.arange(R) - starts[e_s]
            valid = pos < C
            pos_c = jnp.minimum(pos, C - 1)
            xg = jnp.zeros((E, C, D), x.dtype).at[e_s, pos_c].add(jnp.where(valid[:, None], x[tok_s], 0.0))
            h = jax.nn.silu(jnp.einsum('ecd,efd->ecf', xg, w1)) * jnp.einsum('ecd,efd->ecf', xg, v1)
            y = jnp.einsum('ecf,efd->ecd', h, w2)
            yr = y[e_s, pos_c] * jnp.where(valid, w_s, 0.0)[:, None]
            return jnp.zeros((T, D), x.dtype).at[tok_s].add(yr)
        b, s, d = hidden_states.shape
        x = hidden_states.transpose(1, 0, 2).reshape(s * b, d)
        out = _moe(x, router_w, w1, v1, w2)
        return out.reshape(s, b, d).transpose(1, 0, 2)
    x = L0_attn_x
    x = x + 0.5 * _L0_ffn_ref(_layernorm(x, axis=-1), L0_ffn_router_w, L0_ffn_w1, L0_ffn_v1, L0_ffn_w2)
    x = x + _L0_attn_ref(_layernorm(x, axis=-1), L0_attn_Wq, L0_attn_bq, L0_attn_Wk, L0_attn_bk, L0_attn_Wv, L0_attn_bv, L0_attn_Wo, L0_attn_bo)
    x = x + 0.5 * _L0_ffn_ref(_layernorm(x, axis=-1), L0_ffn_router_w, L0_ffn_w1, L0_ffn_v1, L0_ffn_w2)
    return x

_drawn_inputs = setup_inputs


def setup_inputs(seed=0):
    import zlib

    import numpy as np

    out = dict(_drawn_inputs(seed))
    spreads = {'L0_attn_bq': (0.0, 0.733),
     'L0_attn_bk': (0.0, 0.8),
     'L0_attn_bv': (0.0, 0.1),
     'L0_attn_bo': (0.0, 0.1)}
    factors = {'L0_ffn_router_w': 8.0, 'L0_ffn_w1': 8.0, 'L0_ffn_v1': 8.0, 'L0_ffn_w2': 8.0}
    for name, (base, spread) in spreads.items():
        noise = np.random.default_rng([zlib.crc32(name.encode()), seed]).standard_normal(out[name].shape)
        drawn = base * np.exp(spread * noise) if base else spread * noise
        out[name] = jnp.asarray(drawn.astype(out[name].dtype))
    for name, factor in factors.items():
        out[name] = (out[name] * factor).astype(out[name].dtype)
    return out
```

```python
import concourse.bass as bass
from concourse import mybir
from contextlib import ExitStack, contextmanager
import numpy as np

B, S, D = 8, 256, 256
P = 128
T = B * S
TILES = T // P
KD = D // P
H, DH, KV = 16, 128, 4
G = H // KV
E, TOPK, F, C = 64, 8, 96, 32
EG = 4
GROUPS = E // EG
ROW = D + E
BLOCKS = 4
BT = T // BLOCKS
EPS = 1e-5
SCALE = 1.0 / float(np.sqrt(DH))
LOWEST = -3.0e38
WORK_PER_BLOCK = KV * (G + 1) + KD + KV * 4 + 4
SPLITS = KD + 2 + 2


class Tally:

    def __init__(self, sem):
        self.sem, self.fixed, self.turn = sem, 0, None

    def add(self, n=1):
        self.fixed += n
        return self.now()

    def now(self, back=0):
        value = self.fixed - back
        return value if self.turn is None else self.turn + value


@contextmanager
def turns(engine, count, rates):
    with engine.Fori(0, count) as i:
        before = [t.fixed for t, _ in rates]
        for t, per in rates:
            t.turn = i * per
        yield i
        for (t, per), was in zip(rates, before):
            assert t.fixed - was == per, (t.fixed - was, per)
    for t, per in rates:
        t.fixed += per * (count - 1)
        t.turn = None


def macaron_kernel(nc, x_in, wq_in, bq_in, wk_in, bk_in, wv_in, bv_in, wo_in, bo_in, router_in, up_in, down_in, out):
    f32, f32r, i32, u32 = mybir.dt.float32, mybir.dt.float32r, mybir.dt.int32, mybir.dt.uint32
    ALU, ACT, AX = mybir.AluOpType, mybir.ActivationFunctionType, mybir.AxisListType
    ds = bass.ds

    table = nc.dram_tensor("token_table", (T + 1, ROW), f32).ap()

    ctx = ExitStack()
    with ctx:
        def sem(name):
            return ctx.enter_context(nc.semaphore(name))

        def sb(stack, name, shape, dt=f32):
            return stack.enter_context(nc.sbuf_tensor(name, shape, dt))

        x = sb(ctx, "x", [P, TILES, D])
        ident = sb(ctx, "ident", [P, P])
        token_of_column = sb(ctx, "token_of_column", [P, 2, P])
        token_i32 = sb(ctx, "token_i32", [P, 2 * P], i32)
        quadrant = sb(ctx, "quadrant", [P, EG])
        router_w = sb(ctx, "router_w", [P, KD, E])
        bq = sb(ctx, "bq", [P, H])
        bk = sb(ctx, "bk", [P, KV])
        bv = sb(ctx, "bv", [P, KV])
        bo = sb(ctx, "bo", [P, KD])
        stats = sb(ctx, "stats", [P, TILES, 6])
        ln = sb(ctx, "ln", [P, 6, TILES])
        mean, rstd = ln[:, 0, :], ln[:, 1, :]
        slot_token = sb(ctx, "slot_token", [P, GROUPS])
        slot_index = sb(ctx, "slot_index", [P, GROUPS], u32)
        slot_weight = sb(ctx, "slot_weight", [P, GROUPS])
        zero_row = sb(ctx, "zero_row", [1, ROW])
        wq = [sb(ctx, f"wq_{n}", [P, KD, H * DH], f32r) for n in ("hi", "lo")]
        wk = [sb(ctx, f"wk_{n}", [P, KD, KV * DH], f32r) for n in ("hi", "lo")]
        wv = [sb(ctx, f"wv_{n}", [P, KD, KV * DH], f32r) for n in ("hi", "lo")]
        wo = [sb(ctx, f"wo_{n}", [P, H, D], f32r) for n in ("hi", "lo")]

        moe = ExitStack()
        with moe:
            piece = sb(moe, "piece", [P, 2048])
            down_w = sb(moe, "down_w", [F, 2, EG, D])
            with ExitStack() as ring:
                up_w = sb(ring, "up_w", [P, 4, EG, KD, 2 * F])
            with ExitStack() as ring:
                onehot = sb(ring, "onehot", [P, 2, GROUPS, P], f32r)
                sb(ring, "up_w_rest", [P, 2048])
                router = ExitStack()
                with router:
                    xn = sb(router, "xn", [P, TILES, D])
                    xnT = sb(router, "xnT", [P, 2, 2, KD, P])
                    logits = sb(router, "logits", [P, TILES, E])
                    top8 = sb(router, "top8", [P, TILES, 8])
                    struck = sb(router, "struck", [P, TILES, E])
                    chosen = sb(router, "chosen", [P, TILES // 2, 2, E])
                    expw = sb(router, "expw", [P, TILES, E])
                    wsum = sb(router, "wsum", [P, 2, TILES])
                    key_i32 = sb(router, "key_i32", [P, T // 2], i32)
                    key_of_column = sb(router, "key_of_column", [P, T // 2])
                    keys = sb(router, "keys", [P, T // 2])
                    best = sb(router, "best", [P, C])
                    merged = sb(router, "merged", [E, 2 * C])
                    slot_keys = sb(router, "slot_keys", [E, C])
                experts = ExitStack()
                with experts:
                    slots = sb(experts, "slots", [P, GROUPS, ROW])
                    slotsT = sb(experts, "slotsT", [P, 2, KD, P])
                    gate = sb(experts, "gate", [P, 2, F])
                    hidden = sb(experts, "hidden", [P, 2, F])
                    hiddenT = sb(experts, "hiddenT", [F, 2, P])
                    weight4 = sb(experts, "weight4", [P, 2, EG])
                    y_parts = sb(experts, "y_parts", [P, GROUPS, 2, D], f32r)
        with ExitStack() as attention:
            xn4 = sb(attention, "xn4", [P, 4, D])
            xT = [sb(attention, f"xT_{n}", [P, KD, BT], f32r) for n in ("hi", "lo")]
            q = [sb(attention, f"q_{n}", [P, 2, G, BT], f32r) for n in ("hi", "lo")]
            k = [sb(attention, f"k_{n}", [P, 2, BT], f32r) for n in ("hi", "lo")]
            v = [sb(attention, f"v_{n}", [P, 4, KV * DH], f32r) for n in ("hi", "lo")]
            probs = sb(attention, "probs", [P, 2, 4, S])
            probsT = [sb(attention, f"probsT_{n}", [P, 2, 2, S], f32r) for n in ("hi", "lo")]
            o = [sb(attention, f"o_{n}", [P, G, 2, S], f32r) for n in ("hi", "lo")]
            yT = sb(attention, "yT", [P, KD, BT])
            negmax = sb(attention, "negmax", [P, 2, 4])
            rowsum = sb(attention, "rowsum", [P, 2, 4])
            rowinv = sb(attention, "rowinv", [P, 2, 4])

        bank = [ctx.enter_context(nc.psum_tensor(f"bank{n}", [P, 512], f32)) for n in range(8)]
        scores_ps, probsT_ps, work_ps, out_ps = bank[0:2], bank[2:4], bank[4:6], bank[6:8]

        x_loaded = [sem(f"x_loaded{n}") for n in range(4)]
        small_loaded = sem("small_loaded")
        piece_loaded = sem("piece_loaded")
        piece_high = sem("piece_high")
        weights_split = sem("weights_split")
        bq_scaled = sem("bq_scaled")
        constants = sem("constants")
        key_raw = sem("key_raw")
        key_ready = sem("key_ready")
        setup_link = sem("setup_link")
        link = sem("dve_link")
        zero_stored = sem("zero_stored")
        var_ready = sem("var_ready")
        root_ready = sem("root_ready")
        xn_ready = sem("xn_ready")
        xnT_raw = sem("xnT_raw")
        xnT_ready = sem("xnT_ready")
        logits_raw = sem("logits_raw")
        logits_ready = sem("logits_ready")
        top8_ready = sem("top8_ready")
        shifted = sem("shifted")
        exps = sem("exps")
        chosen_ready = sem("chosen_ready")
        masked = sem("masked")
        winv_ready = sem("winv_ready")
        weights_ready = sem("weights_ready")
        chosenT_raw = sem("chosenT_raw")
        first_ready = sem("first_ready")
        slot_raw = sem("slot_raw")
        slot_ready = sem("slot_ready")
        table_written = sem("table_written")
        gathered = [sem(f"gathered{n}") for n in range(4)]
        up_loaded = [sem(f"up_loaded{n}") for n in range(4)]
        down_loaded = [sem(f"down_loaded{n}") for n in range(2)]
        slotsT_raw = sem("slotsT_raw")
        slotsT_ready = sem("slotsT_ready")
        up_done = sem("up_done")
        gate_ready = sem("gate_ready")
        hidden_ready = sem("hidden_ready")
        hiddenT_raw = sem("hiddenT_raw")
        hiddenT_ready = sem("hiddenT_ready")
        down_done = sem("down_done")
        weight_ready = sem("weight_ready")
        y_high = sem("y_high")
        down_free = sem("down_free")
        onehot_ready = sem("onehot_ready")
        combined = sem("combined")
        x_final = sem("x_final")
        out_stored = sem("out_stored")
        xn4_ready = sem("xn4_ready")
        work_ready = sem("work_ready")
        work_high = sem("work_high")
        work_taken = sem("work_taken")
        scores_ready = sem("scores_ready")
        negmax_ready = sem("negmax_ready")
        exp_ready = sem("exp_ready")
        probs_ready = sem("probs_ready")
        probsT_raw = sem("probsT_raw")
        probsT_high = sem("probsT_high")
        probsT_taken = sem("probsT_taken")
        y_raw = sem("y_raw")
        yT_ready = sem("yT_ready")
        y_ready = sem("y_ready")
        y_taken = sem("y_taken")
        attention_done = sem("attention_done")

        def fills(n, last):
            kv, r = divmod(n, 4)
            if last and kv == KV - 1:
                return []
            more = [] if last or n != 11 else [("xT", 0), ("xT", 1)]
            return [[("k", 0), ("q", 0)], [("q", 1), ("q", 2)], [("q", 3)], more][r]

        block = ctx.enter_context(nc.Block())

        @block.sync
        def _(sp):
            for n in range(4):
                sp.dma_start(x[:, 4 * n:4 * n + 4, :],
                             x_in[512 * n:512 * n + 512, :].rearrange("(a p) d -> p a d", p=P)).then_inc(x_loaded[n], 16)
            for dst, src in ((router_w, router_in), (bq, bq_in), (bk, bk_in), (bv, bv_in), (bo, bo_in)):
                sp.dma_start(dst[:], src).then_inc(small_loaded, 16)

            xn_seen, weights_seen = Tally(xn_ready), Tally(weights_ready)
            ups_seen, downs_seen = Tally(up_done), Tally(down_done)

            def load_up(g, slot):
                sp.dma_start(up_w[:, slot, :, :, :], up_in[ds(g * P, P), :].rearrange(
                    "p (j k f) -> p j k f", j=EG, k=KD)).then_inc(up_loaded[slot], 16)

            def load_down(g, slot):
                sp.dma_start(down_w[:, slot, :, :], down_in[ds(g * F, F), :].rearrange(
                    "f (j d) -> f j d", j=EG)).then_inc(down_loaded[slot], 16)

            def expert_layer():
                for g in range(4):
                    load_up(g, g)
                for g in range(2):
                    load_down(g, g)
                rows = table[0:T, :].rearrange("(h p b) e -> h p b e", h=2, p=P)
                for n in range(4):
                    sp.wait_ge(xn_ready, xn_seen.add(4))
                    for half in range(2):
                        sp.dma_start(rows[half, :, 2 * n:2 * n + 2, 0:D],
                                     xn[:, 4 * n + half:4 * n + half + 3:2, :]).then_inc(table_written, 16)
                sp.wait_ge(weights_ready, weights_seen.add())
                for half in range(2):
                    sp.dma_start(rows[half, :, :, D:ROW],
                                 expw[:, half:TILES:2, :]).then_inc(table_written, 16)
                with turns(sp, 3, [(ups_seen, 4), (downs_seen, 4)]) as i:
                    for u in range(4):
                        sp.wait_ge(up_done, ups_seen.add())
                        load_up(i * 4 + u + 4, u)
                        sp.wait_ge(down_done, downs_seen.add())
                        load_down(i * 4 + u + 2, u % 2)
                ups_seen.add(4)
                for u in range(2):
                    sp.wait_ge(down_done, downs_seen.add())
                    load_down(14 + u, u)
                downs_seen.add(2)

            expert_layer()
            sp.wait_ge(attention_done, 1)
            expert_layer()
            final_seen = Tally(x_final)
            final_seen.add(TILES)
            with turns(sp, TILES // 2, [(final_seen, 2)]) as i:
                for u in range(2):
                    sp.wait_ge(x_final, final_seen.add())
                    sp.dma_start(out[ds(i * 2 * P + u * P, P), :],
                                 x[:, ds(i * 2 + u, 1), :].rearrange("p a d -> p (a d)")).then_inc(out_stored, 16)
            sp.wait_ge(out_stored, 16 * TILES)

        @block.gpsimd
        def _(pool):
            nc.gpsimd.memset(ident[:], 0.0).then_inc(setup_link, 1)
            nc.gpsimd.iota(token_i32[:], pattern=[[8, 2 * P]], base=0, channel_multiplier=0).then_inc(setup_link, 1)
            nc.gpsimd.memset(zero_row[:], 0.0).then_inc(setup_link, 1)
            pool.wait_ge(setup_link, 3)
            nc.gpsimd.affine_select(out=ident[:], in_=ident[:], compare_op=ALU.not_equal, fill=1.0, base=0,
                                    pattern=[[-1, P]], channel_multiplier=1).then_inc(constants, 1)
            nc.gpsimd.tensor_copy(token_of_column[:].rearrange("p u r -> p (u r)"), token_i32[:]).then_inc(constants, 1)
            pool.wait_ge(constants, 2)
            pool.dma_start(table[T:T + 1, :], zero_row[0:1, :]).then_inc(zero_stored, 16)

            raw, tops, exp_seen = Tally(key_raw), Tally(top8_ready), Tally(exps)
            masks, inv, slot_seen = Tally(chosen_ready), Tally(winv_ready), Tally(slot_ready)
            written = Tally(table_written)
            arrived = [Tally(s) for s in gathered]

            def expert_layer():
                for half in range(2):
                    nc.gpsimd.iota(key_i32[64 * half:64 * half + 64, :], pattern=[[-1, 4], [-1024, 2], [-8, P]],
                                    base=T - 4 * half, channel_multiplier=0).then_inc(key_raw, 1)
                    pool.wait_ge(key_raw, raw.add())
                nc.gpsimd.tensor_copy(key_of_column[:], key_i32[:]).then_inc(key_ready, 1)
                pool.wait_ge(top8_ready, tops.add())
                nc.gpsimd.tensor_tensor(expw[:], logits[:], top8[:, :, 0:1].to_broadcast([P, TILES, E]),
                                        ALU.subtract).then_inc(shifted, 1)
                pool.wait_ge(chosen_ready, masks.add())
                pool.wait_ge(exps, exp_seen.add())
                nc.gpsimd.tensor_tensor(
                    expw[:].rearrange("p (h i) e -> p h i e", h=2), expw[:].rearrange("p (h i) e -> p h i e", h=2),
                    chosen[:].rearrange("p i h e -> p h i e"), ALU.mult).then_inc(masked, 1)
                pool.wait_ge(winv_ready, inv.add())
                nc.gpsimd.tensor_tensor(expw[:], expw[:], wsum[:, 1, :].unsqueeze(2).to_broadcast([P, TILES, E]),
                                        ALU.mult).then_inc(weights_ready, 1)
                pool.wait_ge(slot_ready, slot_seen.add(2))
                pool.wait_ge(table_written, written.add(160))
                pool.wait_ge(zero_stored, 16)
                for g in range(GROUPS):
                    if g >= 4:
                        pool.wait_ge(gathered[g % 4], arrived[g % 4].now())
                    nc.gpsimd.indirect_dma_start(
                        out=slots[:, g, :], out_offset=None, in_=table[:, :],
                        in_offset=bass.IndirectOffsetOnAxis(ap=slot_index[:, g:g + 1], axis=0),
                    ).then_inc(gathered[g % 4], 16)
                    arrived[g % 4].add(16)

            expert_layer()
            half_wo = H // 2
            jobs = [[(piece[:], wq_in[kd * P:kd * P + P, :], [w[:, kd, :] for w in wq], SCALE)] for kd in range(KD)]
            jobs += [[(piece[:, 1024 * n:1024 * n + 1024].rearrange("p (k n) -> p k n", k=KD),
                       src.rearrange("(k p) n -> p k n", p=P), [w[:] for w in parts], None)
                      for n, (src, parts) in enumerate(((wk_in, wk), (wv_in, wv)))]]
            jobs += [[(piece[:].rearrange("p (h d) -> p h d", d=D),
                       wo_in[n * half_wo * DH:(n + 1) * half_wo * DH, :].rearrange("(h p) d -> p h d", p=P),
                       [w[:, n * half_wo:(n + 1) * half_wo, :] for w in wo], None)] for n in range(2)]
            loads, scaled, parts_done = Tally(piece_loaded), Tally(setup_link), 0
            scaled.add(3)
            for job in jobs:
                if parts_done:
                    pool.wait_ge(weights_split, parts_done)
                for dst, src, _, _ in job:
                    pool.dma_start(dst, src).then_inc(piece_loaded, 16)
                    loads.add(16)
                pool.wait_ge(piece_loaded, loads.now())
                for whole, _, _, scale in job:
                    if scale is not None:
                        nc.gpsimd.tensor_scalar(whole, whole, scale, None, ALU.mult).then_inc(setup_link, 1)
                        pool.wait_ge(setup_link, scaled.add())
                for whole, _, (hi, lo), _ in job:
                    nc.gpsimd.tensor_copy(hi, whole).then_inc(piece_high, 1)
                pool.wait_ge(piece_high, parts_done + len(job))
                for whole, _, (hi, lo), _ in job:
                    nc.gpsimd.tensor_tensor(lo, whole, hi.bitcast(f32), ALU.subtract).then_inc(weights_split, 1)
                parts_done += len(job)
            pool.wait_ge(attention_done, 1)
            expert_layer()

        @block.scalar
        def _(act):
            xnT_seen, logits_seen, shift_seen = Tally(xnT_raw), Tally(logits_raw), Tally(shifted)
            sT_seen, up_seen, hT_seen, down_seen = Tally(slotsT_raw), Tally(up_done), Tally(hiddenT_raw), Tally(down_done)
            weight_seen, vars_seen = Tally(weight_ready), Tally(var_ready)

            def deviations():
                act.wait_ge(var_ready, vars_seen.add())
                nc.scalar.activation(ln[:, 3, :], ln[:, 4, :], ACT.Sqrt).then_inc(root_ready, 1)

            def slot_step(s, parity, nxt, cur, prev):
                if prev:
                    act.wait_ge(hiddenT_raw, hT_seen.add())
                    nc.scalar.copy(hiddenT[:, 1 - parity, :], bank[5 - parity][0:F, 0:P]).then_inc(hiddenT_ready, 1)
                if nxt:
                    act.wait_ge(slotsT_raw, sT_seen.add())
                    nc.scalar.copy(slotsT[:, 1 - parity, :, :].rearrange("p k t -> p (k t)"),
                                   bank[1 - parity][:, 0:KD * P]).then_inc(slotsT_ready, 1)
                if cur:
                    act.wait_ge(up_done, up_seen.add())
                    nc.scalar.activation(gate[:, parity, :], bank[2 + parity][:, 0:F], ACT.Silu).then_inc(gate_ready, 1)
                if prev:
                    act.wait_ge(weight_ready, weight_seen.add())
                    act.wait_ge(down_done, down_seen.add())
                    nc.scalar.activation(y_parts[:, ds(s - 1, 1), 0, :].rearrange("p a d -> p (a d)"), bank[7 - parity][:, 0:D],
                                         ACT.Identity, scale=slot_weight[:, ds(s - 1, 1)]).then_inc(y_high, 1)

            def expert_layer():
                deviations()
                with turns(nc.scalar, 4, [(xnT_seen, 2), (logits_seen, 1)]) as i:
                    for pair in range(2):
                        act.wait_ge(xnT_raw, xnT_seen.add())
                        nc.scalar.copy(xnT[:, pair].rearrange("p t k c -> p (t k c)"), bank[pair][:]).then_inc(xnT_ready, 1)
                    act.wait_ge(logits_raw, logits_seen.add())
                    nc.scalar.copy(logits[:, ds(i * 4, 4), :].rearrange("p t e -> p (t e)"),
                                   bank[2][:, 0:4 * E]).then_inc(logits_ready, 1)
                act.wait_ge(shifted, shift_seen.add())
                nc.scalar.activation(expw[:], expw[:], ACT.Exp).then_inc(exps, 1)
                act.wait_ge(slotsT_raw, sT_seen.add())
                nc.scalar.copy(slotsT[:, 0, :, :].rearrange("p k t -> p (k t)"), bank[0][:, 0:KD * P]).then_inc(slotsT_ready, 1)
                slot_step(0, 0, True, True, False)
                with turns(nc.scalar, 3, [(hT_seen, 4), (sT_seen, 4), (up_seen, 4), (weight_seen, 4), (down_seen, 4)]) as i:
                    for u in range(4):
                        slot_step(i * 4 + 1 + u, (1 + u) % 2, True, True, True)
                for s in range(13, GROUPS + 1):
                    slot_step(s, s % 2, s < GROUPS - 1, s < GROUPS, True)

            expert_layer()

            work_seen, pT_seen = Tally(work_ready), Tally(probsT_raw)
            scores_seen, max_seen, y_seen = Tally(scores_ready), Tally(negmax_ready), Tally(y_raw)
            uses = [0]

            def take_high(dst, bias=None):
                act.wait_ge(work_ready, work_seen.add())
                src = work_ps[uses[0] % 2]
                uses[0] += 1
                src = src[:] if dst.ndim == 2 else src[:].rearrange("p (h s) -> p h s", h=2)
                if bias is None:
                    nc.scalar.copy(dst, src).then_inc(work_high, 1)
                else:
                    nc.scalar.activation(dst, src, ACT.Identity, bias=bias).then_inc(work_high, 1)

            def take_fill(what, n, kv):
                if what == "k":
                    take_high(k[0][:, kv % 2, :], bk[:, kv:kv + 1])
                elif what == "q":
                    take_high(q[0][:, kv % 2, n, :], bq[:, G * kv + n:G * kv + n + 1])
                else:
                    take_high(xT[0][:, n, :])

            def exps_of(n, head):
                act.wait_ge(scores_ready, scores_seen.add())
                act.wait_ge(negmax_ready, max_seen.add())
                for qt in range(2):
                    t = 2 * head + qt
                    nc.scalar.activation(probs[:, n % 2, t, :], scores_ps[head][:, qt * S:qt * S + S], ACT.Exp,
                                         bias=negmax[:, n % 2, t:t + 1],
                                         accum_out=rowsum[:, n % 2, t:t + 1]).then_inc(exp_ready, 1)

            def steps(last):
                for n in range(16):
                    kv, r = divmod(n, 4)
                    bb, hp = divmod(r, 2)
                    for head in range(2):
                        act.wait_ge(probsT_raw, pT_seen.add())
                        nc.scalar.copy(probsT[0][:, head].rearrange("p c s -> p (c s)"),
                                       probsT_ps[head][:]).then_inc(probsT_high, 1)
                    more = list(fills(n, last))
                    for head in range(2):
                        if not (last and n == 15):
                            exps_of(n + 1, head)
                        if more:
                            take_fill(*more.pop(0), (kv + 1) % KV)
                    take_high(o[0][:, 2 * hp:2 * hp + 2, bb, :], bv[:, kv:kv + 1])
                if not last:
                    for t in range(4):
                        take_high(v[0][:, t, :])
                act.wait_ge(y_raw, y_seen.add())
                for d in range(KD):
                    nc.scalar.activation(yT[:, d, :], out_ps[d][:], ACT.Identity, bias=bo[:, d:d + 1]).then_inc(yT_ready, 1)

            act.wait_ge(small_loaded, 80)
            act.wait_ge(bq_scaled, 1)
            deviations()
            for n in range(KD):
                take_fill("xT", n, 0)
            for t in range(4):
                take_high(v[0][:, t, :])
            for what, n in [("k", 0)] + [("q", g) for g in range(G)]:
                take_fill(what, n, 0)
            for head in range(2):
                exps_of(0, head)
            with turns(nc.scalar, BLOCKS - 1, [(work_seen, WORK_PER_BLOCK), (pT_seen, 32), (scores_seen, 32),
                                               (max_seen, 32), (y_seen, 1)]):
                steps(False)
            steps(True)
            expert_layer()

        @block.vector
        def _(dve):
            linked = Tally(link)

            def tie(ins):
                ins.then_inc(link, 1)
                dve.wait_ge(link, linked.add())

            nc.vector.sem_inc(down_free, 2)
            nc.vector.sem_inc(y_taken, 2)
            tie(nc.vector.memset(quadrant[:], 0.0))
            for j in range(EG):
                last = nc.vector.memset(quadrant[32 * j:32 * j + 32, j:j + 1], 1.0)
            tie(last)
            logits_seen, key_seen, pairs_seen = Tally(logits_ready), Tally(key_ready), Tally(chosenT_raw)
            masked_seen, slot_seen, gates_seen = Tally(masked), Tally(slot_raw), Tally(gate_ready)
            high_seen, combined_seen = Tally(y_high), Tally(combined)
            arrived = [Tally(s) for s in gathered]
            roots_seen = Tally(root_ready)

            def layer_norm_stats(first):
                for a in range(TILES):
                    if first and a % 4 == 0:
                        dve.wait_ge(x_loaded[a // 4], 16)
                    last = nc.vector.bn_stats(stats[:, a, :], x[:, a, :])
                tie(last)
                even, odd = stats[:, :, 1], stats[:, :, 4]
                half_gap, gap2, var = ln[:, 2, :], ln[:, 3, :], ln[:, 4, :]
                nc.vector.tensor_tensor(mean, even, odd, ALU.add)
                nc.vector.tensor_tensor(var, stats[:, :, 2], stats[:, :, 5], ALU.add)
                tie(nc.vector.tensor_tensor(half_gap, even, odd, ALU.subtract))
                tie(nc.vector.scalar_tensor_tensor(gap2, half_gap, 0.25, half_gap, ALU.mult, ALU.mult))
                nc.vector.tensor_scalar(mean, mean, 0.5, None, ALU.mult)
                tie(nc.vector.scalar_tensor_tensor(var, var, 1.0 / D, gap2, ALU.mult, ALU.add))
                nc.vector.tensor_scalar(var, var, EPS, None, ALU.add).then_inc(var_ready, 1)
                dve.wait_ge(root_ready, roots_seen.add())
                tie(nc.vector.reciprocal(rstd, gap2))
                tie(nc.vector.tensor_tensor(gap2, rstd, rstd, ALU.mult))
                tie(nc.vector.tensor_tensor(gap2, gap2, var, ALU.mult))
                tie(nc.vector.tensor_scalar(gap2, gap2, -0.5, 1.5, ALU.mult, ALU.add))
                tie(nc.vector.tensor_tensor(rstd, rstd, gap2, ALU.mult))

            def slot_step(s, parity, u, cur, prev):
                if cur:
                    dve.wait_ge(gathered[u], arrived[u].add(16))
                    tie(nc.vector.tensor_tensor(weight4[:, parity, :], slots[:, ds(s, 1), ds(s + D, EG, step=GROUPS)].rearrange(
                        "p a e -> p (a e)"), quadrant[:], ALU.mult))
                    nc.vector.tensor_reduce(slot_weight[:, ds(s, 1)], weight4[:, parity, :], AX.X, ALU.add).then_inc(weight_ready, 1)
                    dve.wait_ge(gate_ready, gates_seen.add())
                    nc.vector.tensor_tensor(hidden[:, parity, :], gate[:, parity, :], bank[2 + parity][:, F:2 * F],
                                            ALU.mult).then_inc(hidden_ready, 1)
                if prev:
                    dve.wait_ge(y_high, high_seen.add())
                    nc.vector.scalar_tensor_tensor(
                        y_parts[:, ds(s - 1, 1), 1, :].rearrange("p a d -> p (a d)"), bank[7 - parity][:, 0:D],
                        slot_weight[:, ds(s - 1, 1)],
                        y_parts[:, ds(s - 1, 1), 0, :].rearrange("p a d -> p (a d)").bitcast(f32),
                        ALU.mult, ALU.subtract).then_inc(down_free, 1)

            def expert_layer(first):
                layer_norm_stats(first)
                for a in range(TILES):
                    nc.vector.tensor_scalar(xn[:, a, :], x[:, a, :], mean[:, a:a + 1], rstd[:, a:a + 1],
                                            ALU.subtract, ALU.mult).then_inc(xn_ready, 1)
                for a in range(TILES):
                    if a % 4 == 0:
                        dve.wait_ge(logits_ready, logits_seen.add())
                    last = nc.vector.max(top8[:, a, :], logits[:, a, :])
                last.then_inc(top8_ready, 1)
                dve.wait_ge(top8_ready, 1 if first else 2)
                for a in range(TILES):
                    last = nc.vector.match_replace(struck[:, a, :], top8[:, a, :], logits[:, a, :], LOWEST)
                tie(last)
                nc.vector.tensor_scalar(chosen[:].rearrange("p i h e -> p h i e"),
                                        struck[:].rearrange("p (h i) e -> p h i e", h=2), 0.99 * LOWEST, None,
                                        ALU.is_lt).then_inc(chosen_ready, 1)
                dve.wait_ge(key_ready, key_seen.add())
                for n in range(2):
                    dve.wait_ge(chosenT_raw, pairs_seen.add())
                    last = nc.vector.tensor_tensor(keys[:, 512 * n:512 * n + 512], bank[n][:],
                                                   key_of_column[:, 512 * n:512 * n + 512], ALU.mult)
                tie(last)
                for n in range(C // 8):
                    tie(nc.vector.max(best[:, 8 * n:8 * n + 8], keys[:]))
                    if n < C // 8 - 1:
                        tie(nc.vector.match_replace(keys[:], best[:, 8 * n:8 * n + 8], keys[:], -1.0))
                    if n == 1:
                        dve.wait_ge(masked, masked_seen.add())
                        tie(nc.vector.tensor_reduce(wsum[:, 0, :], expw[:], AX.X, ALU.add))
                        tie(nc.vector.reciprocal(wsum[:, 1, :], wsum[:, 0, :]))
                        nc.vector.tensor_scalar(wsum[:, 1, :], wsum[:, 1, :], 0.5, None, ALU.mult).then_inc(winv_ready, 1)
                nc.vector.tensor_copy(merged[:, 0:C], best[0:E, :])
                tie(nc.vector.tensor_copy(merged[:, C:2 * C], best[E:P, :]))
                for n in range(C // 8):
                    last = nc.vector.max(first_keys(n), merged[:])
                    if n < C // 8 - 1:
                        tie(last)
                        tie(nc.vector.match_replace(merged[:], first_keys(n), merged[:], -1.0))
                last.then_inc(first_ready, 1)
                dve.wait_ge(slot_raw, slot_seen.add())
                for dst in (slot_token, slot_index):
                    nc.vector.tensor_scalar(dst[:], bank[4][:, 0:GROUPS], -1.0, float(T), ALU.mult, ALU.add).then_inc(slot_ready, 1)

                slot_step(0, 0, 0, True, False)
                with turns(nc.vector, 3, [(linked, 4), (gates_seen, 4), (high_seen, 4)] + [(t, 16) for t in arrived]) as i:
                    for u in range(4):
                        slot_step(i * 4 + 1 + u, (1 + u) % 2, (1 + u) % 4, True, True)
                for s in range(13, GROUPS + 1):
                    slot_step(s, s % 2, s % 4, s < GROUPS, True)

                dve.wait_ge(slot_ready, 2 if first else 4)

                def mark(u):
                    nc.vector.tensor_tensor(onehot[:, u, :, :], token_of_column[:, u:u + 1, :].to_broadcast([P, GROUPS, P]),
                                            slot_token[:].unsqueeze(2).to_broadcast([P, GROUPS, P]),
                                            ALU.is_equal).then_inc(onehot_ready, 1)

                def add(a, u):
                    dve.wait_ge(combined, combined_seen.add())
                    xa = x[:, ds(a, 1), :].rearrange("p a d -> p (a d)")
                    tie(nc.vector.tensor_tensor(xa, xa, bank[u][:, 0:D], ALU.add))
                    nc.vector.tensor_tensor(xa, xa, bank[u][:, D:2 * D], ALU.add).then_inc(x_final, 1)

                mark(0)
                with turns(nc.vector, TILES // 2 - 1, [(linked, 3), (combined_seen, 2)]) as i:
                    mark(1)
                    add(i * 2, 0)
                    tie(nc.vector.tensor_scalar(slot_token[:], slot_token[:], -1.0, None, ALU.add))
                    mark(0)
                    add(i * 2 + 1, 1)
                mark(1)
                add(TILES - 2, 0)
                add(TILES - 1, 1)
                dve.wait_ge(x_final, TILES if first else 2 * TILES)

            def first_keys(n):
                return slot_keys[:, 8 * n:8 * n + 8]

            expert_layer(True)
            dve.wait_ge(small_loaded, 80)
            nc.vector.tensor_scalar(bq[:], bq[:], SCALE, None, ALU.mult).then_inc(bq_scaled, 1)
            dve.wait_ge(bq_scaled, 1)

            high_work, pT_high = Tally(work_high), Tally(probsT_high)
            scores_seen, exp_seen, y_seen = Tally(scores_ready), Tally(exp_ready), Tally(y_ready)
            uses = [0]

            def normalise_tokens(i):
                for t in range(4):
                    a = i * 4 + t if isinstance(i, int) else i * 4 + (t + 4)
                    last = nc.vector.tensor_scalar(xn4[:, t, :], x[:, ds(a, 1), :].rearrange("p a d -> p (a d)"),
                                                   mean[:, ds(a, 1)], rstd[:, ds(a, 1)], ALU.subtract, ALU.mult)
                last.then_inc(xn4_ready, 1)

            def take_low(hi, lo, bias=None):
                dve.wait_ge(work_high, high_work.add())
                src = work_ps[uses[0] % 2]
                uses[0] += 1
                src = src[:] if hi.ndim == 2 else src[:].rearrange("p (h s) -> p h s", h=2)
                if bias is None:
                    nc.vector.tensor_tensor(lo, src, hi.bitcast(f32), ALU.subtract).then_inc(work_taken, 1)
                else:
                    nc.vector.scalar_tensor_tensor(lo, src, bias, hi.bitcast(f32), ALU.add, ALU.subtract).then_inc(work_taken, 1)

            def take_fill(what, n, kv):
                if what == "k":
                    take_low(*[t[:, kv % 2, :] for t in k], bk[:, kv:kv + 1])
                elif what == "q":
                    take_low(*[t[:, kv % 2, n, :] for t in q], bq[:, G * kv + n:G * kv + n + 1])
                else:
                    take_low(*[t[:, n, :] for t in xT])

            def maxima(n):
                for head in range(2):
                    dve.wait_ge(scores_ready, scores_seen.add())
                    nc.vector.reduce_max(negmax[:, n % 2, 2 * head:2 * head + 2],
                                         scores_ps[head][:].rearrange("p (t s) -> p t s", t=2), AX.X,
                                         negate=True).then_inc(negmax_ready, 1)

            def normalise_probs(n):
                dve.wait_ge(exp_ready, exp_seen.add(4))
                tie(nc.vector.reciprocal(rowinv[:, n % 2, :], rowsum[:, n % 2, :]))
                for t in range(4):
                    last = nc.vector.tensor_scalar(probs[:, n % 2, t, :], probs[:, n % 2, t, :],
                                                   rowinv[:, n % 2, t:t + 1], None, ALU.mult)
                last.then_inc(probs_ready, 1)

            def steps(i, last):
                for n in range(16):
                    kv, r = divmod(n, 4)
                    bb, hp = divmod(r, 2)
                    for head in range(2):
                        dve.wait_ge(probsT_high, pT_high.add())
                        nc.vector.tensor_tensor(probsT[1][:, head].rearrange("p c s -> p (c s)"), probsT_ps[head][:],
                                                probsT[0][:, head].rearrange("p c s -> p (c s)").bitcast(f32),
                                                ALU.subtract).then_inc(probsT_taken, 1)
                    if not (last and n == 15):
                        maxima(n + 1)
                    for what, m in fills(n, last):
                        take_fill(what, m, (kv + 1) % KV)
                    if n == 9 and not last:
                        normalise_tokens(i)
                    if not (last and n == 15):
                        normalise_probs(n + 1)
                    take_low(*[t[:, 2 * hp:2 * hp + 2, bb, :] for t in o], bv[:, kv:kv + 1])
                if not last:
                    for t in range(4):
                        take_low(*[w[:, t, :] for w in v])
                for pair in range(2):
                    dve.wait_ge(y_ready, y_seen.add())
                    xa = x[:, ds(i * 4 + 2 * pair, 2), :].rearrange("p t d -> p (t d)")
                    last_add = nc.vector.tensor_tensor(xa, xa, probsT_ps[pair][:], ALU.add)
                    last_add.then_inc(y_taken, 1)

            layer_norm_stats(False)
            dve.wait_ge(weights_split, SPLITS)
            normalise_tokens(0)
            for n in range(KD):
                take_fill("xT", n, 0)
            for t in range(4):
                take_low(*[w[:, t, :] for w in v])
            for what, n in [("k", 0)] + [("q", g) for g in range(G)]:
                take_fill(what, n, 0)
            maxima(0)
            normalise_probs(0)
            with turns(nc.vector, BLOCKS - 1, [(linked, 16), (high_work, WORK_PER_BLOCK), (pT_high, 32),
                                               (scores_seen, 32), (exp_seen, 64), (y_seen, 2)]) as i:
                steps(i, False)
            steps(BLOCKS - 1, True)
            dve.wait_ge(y_taken, 2 + 2 * BLOCKS)
            nc.vector.sem_inc(attention_done, 1)
            expert_layer(False)

        @block.tensor
        def _(pe):
            mm = nc.tensor.matmul
            xn_seen, xnT_seen, logits_taken = Tally(xn_ready), Tally(xnT_ready), Tally(logits_ready)
            chosen_seen, keys_seen = Tally(chosen_ready), Tally(first_ready)
            arrived = [Tally(s) for s in gathered]
            up_in_seen, down_in_seen = [Tally(s) for s in up_loaded], [Tally(s) for s in down_loaded]
            sT_seen, hidden_seen, hT_seen = Tally(slotsT_ready), Tally(hidden_ready), Tally(hiddenT_ready)
            free_seen, hot_seen = Tally(down_free), Tally(onehot_ready)

            def transpose_slots(s, parity, u):
                pe.wait_ge(gathered[u], arrived[u].add(16))
                for kd in range(KD):
                    last = nc.tensor.transpose(bank[parity][:, kd * P:kd * P + P],
                                               slots[:, s, kd * P:kd * P + P], ident[:])
                last.then_inc(slotsT_raw, 1)

            def slot_step(s, parity, nxt, cur, prev):
                if prev:
                    pe.wait_ge(hidden_ready, hidden_seen.add())
                    nc.tensor.transpose(bank[5 - parity][0:F, 0:P], hidden[:, 1 - parity, :], ident[:]).then_inc(hiddenT_raw, 1)
                if nxt:
                    transpose_slots(s + 1, 1 - parity, (s + 1) % 4)
                if cur:
                    pe.wait_ge(slotsT_ready, sT_seen.add())
                    pe.wait_ge(up_loaded[s % 4], up_in_seen[s % 4].add(16))
                    for kd in range(KD):
                        for j in range(EG):
                            last = mm(bank[2 + parity][32 * j:32 * j + 32, 0:2 * F], slotsT[:, parity, kd, 32 * j:32 * j + 32],
                                      up_w[:, s % 4, j, kd, :], start=kd == 0, stop=kd == KD - 1, tile_position=(0, 32 * j))
                    last.then_inc(up_done, 1)
                if prev:
                    pe.wait_ge(hiddenT_ready, hT_seen.add())
                    pe.wait_ge(down_loaded[1 - parity], down_in_seen[1 - parity].add(16))
                    pe.wait_ge(down_free, free_seen.add())
                    for j in range(EG):
                        last = mm(bank[7 - parity][32 * j:32 * j + 32, 0:D], hiddenT[:, 1 - parity, 32 * j:32 * j + 32],
                                  down_w[:, 1 - parity, j, :], start=True, stop=True, tile_position=(0, 32 * j))
                    last.then_inc(down_done, 1)

            def expert_layer(first):
                for n in range(4):
                    for pair in range(2):
                        pe.wait_ge(xn_ready, xn_seen.add(2))
                        for t in range(2):
                            for kd in range(KD):
                                c = (2 * t + kd) * P
                                last = nc.tensor.transpose(bank[pair][:, c:c + P],
                                                           xn[:, 4 * n + 2 * pair + t, kd * P:kd * P + P], ident[:])
                        last.then_inc(xnT_raw, 1)
                    for pair in range(2):
                        pe.wait_ge(xnT_ready, xnT_seen.add())
                        if pair == 0 and logits_taken.now() > 0:
                            pe.wait_ge(logits_ready, logits_taken.now())
                        for t in range(2):
                            for kd in range(KD):
                                last = mm(bank[2][:, (2 * pair + t) * E:(2 * pair + t + 1) * E], xnT[:, pair, t, kd, :],
                                          router_w[:, kd, :], start=kd == 0, stop=kd == KD - 1)
                    last.then_inc(logits_raw, 1)
                    logits_taken.add()
                pe.wait_ge(chosen_ready, chosen_seen.add())
                for n in range(2):
                    for c in range(4):
                        last = nc.tensor.transpose(bank[n][:, c * P:c * P + P],
                                                   chosen[:, 4 * n + c, :, :].rearrange("p h e -> p (h e)"), ident[:])
                    last.then_inc(chosenT_raw, 1)
                pe.wait_ge(first_ready, keys_seen.add())
                for j in range(EG):
                    last = mm(bank[4][32 * j:32 * j + 32, 0:GROUPS], slot_keys[:], ident[0:E, GROUPS * j:GROUPS * j + GROUPS],
                              start=True, stop=True, tile_position=(0, 32 * j))
                last.then_inc(slot_raw, 1)
                transpose_slots(0, 0, 0)
                for s in range(GROUPS + 1):
                    slot_step(s, s % 2, s < GROUPS - 1, s < GROUPS, s > 0)
                pe.wait_ge(down_free, free_seen.now() + 2)

                with turns(nc.tensor, TILES // 2, [(hot_seen, 2)]) as i:
                    for u in range(2):
                        pe.wait_ge(onehot_ready, hot_seen.add())
                        for g in range(GROUPS):
                            last = mm(bank[u][:], onehot[:, u, g, :], y_parts[:, g, :, :].rearrange("p a d -> p (a d)"),
                                      start=g == 0, stop=g == GROUPS - 1)
                        last.then_inc(combined, 1)

            pe.wait_ge(constants, 2)
            pe.wait_ge(small_loaded, 80)
            expert_layer(True)

            taken, xn4_seen, pT_taken = Tally(work_taken), Tally(xn4_ready), Tally(probsT_taken)
            probs_seen, yT_seen, y_out = Tally(probs_ready), Tally(yT_ready), Tally(y_taken)
            uses = [0]
            issued = Tally(work_taken)

            def work():
                if not (issued.turn is None and issued.fixed < 2):
                    pe.wait_ge(work_taken, issued.now(back=1))
                issued.add()
                uses[0] += 1
                return work_ps[(uses[0] - 1) % 2]

            def three(dst, w, m, start, stop):
                mm(dst, w[0], m[0], start=start, stop=False)
                mm(dst, w[0], m[1], start=False, stop=False)
                return mm(dst, w[1], m[0], start=False, stop=stop)

            def project(what, n, kv):
                ps = work()
                if what == "xT":
                    for t in range(4):
                        last = nc.tensor.transpose(ps[:, t * P:t * P + P], xn4[:, t, n * P:n * P + P], ident[:])
                else:
                    w, c = (wk, kv * DH) if what == "k" else (wq, (G * kv + n) * DH)
                    for kd in range(KD):
                        last = three(ps[:], [a[:, kd, c:c + DH] for a in w], [a[:, kd, :] for a in xT], kd == 0, kd == KD - 1)
                last.then_inc(work_ready, 1)

            def project_v():
                for t in range(4):
                    ps = work()
                    for kd in range(KD):
                        last = three(ps[:], [a[:, kd, t * P:t * P + P] for a in xT], [a[:, kd, :] for a in wv], kd == 0, kd == KD - 1)
                    last.then_inc(work_ready, 1)

            def scores(n):
                kv, r = divmod(n % 16, 4)
                bb, hp = divmod(r, 2)
                for head in range(2):
                    for qt in range(2):
                        c = bb * S + qt * P
                        last = three(scores_ps[head][:, qt * S:qt * S + S], [a[:, kv % 2, 2 * hp + head, c:c + P] for a in q],
                                     [a[:, kv % 2, bb * S:bb * S + S] for a in k], True, True)
                    last.then_inc(scores_ready, 1)

            def steps(i, last_block):
                for n in range(16):
                    kv, r = divmod(n, 4)
                    bb, hp = divmod(r, 2)
                    if n == 0:
                        pe.wait_ge(y_taken, y_out.now(back=-2))
                    pe.wait_ge(probs_ready, probs_seen.add())
                    for head in range(2):
                        for qt in range(2):
                            for c in range(2):
                                last = nc.tensor.transpose(probsT_ps[head][:, c * S + qt * P:c * S + qt * P + P],
                                                           probs[:, n % 2, 2 * head + qt, c * P:c * P + P], ident[:])
                        last.then_inc(probsT_raw, 1)
                    if not (last_block and n == 15):
                        if r == 3:
                            pe.wait_ge(work_taken, issued.now(back=1))
                        scores(n + 1)
                    if n == 11 and not last_block:
                        pe.wait_ge(xn4_ready, xn4_seen.add())
                    for what, m in fills(n, last_block):
                        if n == 12 and what == "k":
                            pe.wait_ge(work_taken, issued.now(back=1))
                        project(what, m, (kv + 1) % KV)
                    if r == 0 and kv > 0:
                        project_out(kv - 1, len(fills(n, last_block)))
                    pe.wait_ge(probsT_taken, pT_taken.add(2))
                    if n == 0:
                        pe.wait_ge(work_taken, issued.now(back=2))
                    ps = work()
                    for c in range(2):
                        last = three(ps[:].rearrange("p (h s) -> p h s", h=2), [a[:, 2 * bb + c, kv * DH:kv * DH + DH] for a in v],
                                     [a[:, :, c, :] for a in probsT], c == 0, c == 1)
                    last.then_inc(work_ready, 1)
                if not last_block:
                    project_v()
                project_out(KV - 1, 0 if last_block else 4)
                yT_seen.add(KD)
                pe.wait_ge(yT_ready, yT_seen.now())
                for pair in range(2):
                    for t in range(2):
                        for d in range(KD):
                            c = (2 * pair + t) * P
                            last = nc.tensor.transpose(probsT_ps[pair][:, t * D + d * P:t * D + d * P + P],
                                                       yT[:, d, c:c + P], ident[:])
                    last.then_inc(y_ready, 1)
                y_out.add(2)

            def project_out(kv, since):
                pe.wait_ge(work_taken, issued.now(back=since))
                for d in range(KD):
                    for g in range(G):
                        last = three(out_ps[d][:], [a[:, G * kv + g, d * P:d * P + P] for a in wo],
                                     [a[:, g, :, :].rearrange("p b s -> p (b s)") for a in o],
                                     kv == 0 and g == 0, kv == KV - 1 and g == G - 1)
                if kv == KV - 1:
                    last.then_inc(y_raw, 1)

            pe.wait_ge(weights_split, SPLITS)
            pe.wait_ge(xn4_ready, xn4_seen.add())
            for n in range(KD):
                project("xT", n, 0)
            pe.wait_ge(work_taken, issued.now())
            project_v()
            for what, n in [("k", 0)] + [("q", g) for g in range(G)]:
                project(what, n, 0)
            pe.wait_ge(work_taken, issued.now())
            scores(0)
            with turns(nc.tensor, BLOCKS - 1, [(issued, WORK_PER_BLOCK), (xn4_seen, 1), (pT_taken, 32), (probs_seen, 16),
                                               (yT_seen, KD), (y_out, 2)]) as i:
                steps(i, False)
            steps(BLOCKS - 1, True)
            expert_layer(False)


def kernel(L0_attn_x, L0_attn_Wq, L0_attn_bq, L0_attn_Wk, L0_attn_bk, L0_attn_Wv, L0_attn_bv, L0_attn_Wo, L0_attn_bo,
           L0_ffn_router_w, L0_ffn_w1, L0_ffn_v1, L0_ffn_w2):
    import concourse.bacc as bacc
    from concourse.bass_utils import run_bass_kernel_spmd

    def arr(a):
        return np.ascontiguousarray(a)

    up = np.concatenate([np.asarray(L0_ffn_w1), np.asarray(L0_ffn_v1)], axis=1)
    up = up.reshape(EG, GROUPS, 2 * F, KD, P).transpose(1, 4, 0, 3, 2).reshape(GROUPS * P, EG * KD * 2 * F)
    down = np.asarray(L0_ffn_w2).reshape(EG, GROUPS, F, D).transpose(1, 2, 0, 3).reshape(GROUPS * F, EG * D)
    arrays = {
        "x_in": arr(np.asarray(L0_attn_x).reshape(T, D)),
        "wq_in": arr(L0_attn_Wq), "bq_in": arr(np.asarray(L0_attn_bq).reshape(H, DH).T),
        "wk_in": arr(L0_attn_Wk), "bk_in": arr(np.asarray(L0_attn_bk).reshape(KV, DH).T),
        "wv_in": arr(L0_attn_Wv), "bv_in": arr(np.asarray(L0_attn_bv).reshape(KV, DH).T),
        "wo_in": arr(L0_attn_Wo), "bo_in": arr(np.asarray(L0_attn_bo).reshape(KD, P).T),
        "router_in": arr(np.asarray(L0_ffn_router_w).reshape(E, KD, P).transpose(2, 1, 0)),
        "up_in": arr(up), "down_in": arr(down),
    }
    nc = bacc.Bacc("TRN2", target_bir_lowering=False, num_devices=1)
    args = [nc.dram_tensor(n, a.shape, mybir.dt.from_np(a.dtype), kind="ExternalInput").ap() for n, a in arrays.items()]
    result = nc.dram_tensor("out", (T, D), mybir.dt.float32, kind="ExternalOutput").ap()
    macaron_kernel(nc, *args, result)
    r = run_bass_kernel_spmd(nc, [arrays], core_ids=[0])
    return r.results[0]["out"].reshape(B, S, D)
```

```python
import concourse.bass as bass
from concourse import mybir
from contextlib import ExitStack, contextmanager
import numpy as np

B, S, D = 8, 256, 256
P = 128
T = B * S
TILES = T // P
KD = D // P
H, DH, KV = 16, 128, 4
G = H // KV
E, TOPK, F, C = 64, 8, 96, 32
EG = 4
GROUPS = E // EG
ROW = D + E
BLOCKS = 4
BT = T // BLOCKS
EPS = 1e-5
SCALE = 1.0 / float(np.sqrt(DH))
LOWEST = -3.0e38
STEPS = 16
WORK_PER_BLOCK = KV * (G + 1) + KD + STEPS + 4 + 2
SPLITS = KD + 2 + 2


class Tally:

    def __init__(self, sem):
        self.sem, self.fixed, self.turn = sem, 0, None

    def add(self, n=1):
        self.fixed += n
        return self.now()

    def now(self, back=0):
        value = self.fixed - back
        return value if self.turn is None else self.turn + value


@contextmanager
def turns(engine, count, rates):
    with engine.Fori(0, count) as i:
        before = [t.fixed for t, _ in rates]
        for t, per in rates:
            t.turn = i * per
        yield i
        for (t, per), was in zip(rates, before):
            assert t.fixed - was == per, (t.fixed - was, per)
    for t, per in rates:
        t.fixed += per * (count - 1)
        t.turn = None


def macaron_kernel(nc, x_in, wq_in, bq_in, wk_in, bk_in, wv_in, bv_in, wo_in, bo_in, router_in, up_in, down_in, out):
    f32, f32r, i32, u32 = mybir.dt.float32, mybir.dt.float32r, mybir.dt.int32, mybir.dt.uint32
    ALU, ACT, AX = mybir.AluOpType, mybir.ActivationFunctionType, mybir.AxisListType
    ds = bass.ds

    table = nc.dram_tensor("token_table", (T + 1, ROW), f32).ap()

    ctx = ExitStack()
    with ctx:
        def sem(name):
            return ctx.enter_context(nc.semaphore(name))

        def sb(stack, name, shape, dt=f32):
            return stack.enter_context(nc.sbuf_tensor(name, shape, dt))

        x = sb(ctx, "x", [P, TILES, D])
        ident = sb(ctx, "ident", [P, P])
        token_of_column = sb(ctx, "token_of_column", [P, 2, P])
        token_i32 = sb(ctx, "token_i32", [P, 2 * P], i32)
        quadrant = sb(ctx, "quadrant", [P, EG])
        router_w = sb(ctx, "router_w", [P, KD, E])
        bq = sb(ctx, "bq", [P, H])
        bk = sb(ctx, "bk", [P, KV])
        bv = sb(ctx, "bv", [P, KV])
        bo = sb(ctx, "bo", [P, KD])
        stats = sb(ctx, "stats", [P, TILES, 6])
        ln = sb(ctx, "ln", [P, 6, TILES])
        mean, rstd = ln[:, 0, :], ln[:, 1, :]
        slot_token = sb(ctx, "slot_token", [P, GROUPS])
        slot_index = sb(ctx, "slot_index", [P, GROUPS], u32)
        slot_weight = sb(ctx, "slot_weight", [P, GROUPS])
        zero_row = sb(ctx, "zero_row", [1, ROW])
        wq = [sb(ctx, f"wq_{n}", [P, KD, H * DH], f32r) for n in ("hi", "lo")]
        wk = [sb(ctx, f"wk_{n}", [P, KD, KV * DH], f32r) for n in ("hi", "lo")]
        wv = [sb(ctx, f"wv_{n}", [P, KD, KV * DH], f32r) for n in ("hi", "lo")]
        wo = [sb(ctx, f"wo_{n}", [P, H, D], f32r) for n in ("hi", "lo")]

        moe = ExitStack()
        with moe:
            piece = sb(moe, "piece", [P, 2048])
            down_w = sb(moe, "down_w", [F, 2, EG, D])
            with ExitStack() as ring:
                up_w = sb(ring, "up_w", [P, 4, EG, KD, 2 * F])
            with ExitStack() as ring:
                onehot = sb(ring, "onehot", [P, 2, GROUPS, P], f32r)
                sb(ring, "up_w_rest", [P, 2048])
                router = ExitStack()
                with router:
                    xn = sb(router, "xn", [P, TILES, D])
                    xnT = sb(router, "xnT", [P, 2, 2, KD, P])
                    logits = sb(router, "logits", [P, TILES, E])
                    top8 = sb(router, "top8", [P, TILES, 8])
                    struck = sb(router, "struck", [P, TILES, E])
                    chosen = sb(router, "chosen", [P, TILES // 2, 2, E])
                    expw = sb(router, "expw", [P, TILES, E])
                    wsum = sb(router, "wsum", [P, 2, TILES])
                    key_i32 = sb(router, "key_i32", [P, T // 2], i32)
                    key_of_column = sb(router, "key_of_column", [P, T // 2])
                    keys = sb(router, "keys", [P, T // 2])
                    best = sb(router, "best", [P, C])
                    merged = sb(router, "merged", [E, 2 * C])
                    slot_keys = sb(router, "slot_keys", [E, C])
                experts = ExitStack()
                with experts:
                    slots = sb(experts, "slots", [P, GROUPS, ROW])
                    slotsT = sb(experts, "slotsT", [P, 2, KD, P])
                    gate = sb(experts, "gate", [P, 2, F])
                    hidden = sb(experts, "hidden", [P, 2, F])
                    hiddenT = sb(experts, "hiddenT", [F, 2, P])
                    weight4 = sb(experts, "weight4", [P, 2, EG])
                    y_parts = sb(experts, "y_parts", [P, GROUPS, 2, D], f32r)
        with ExitStack() as attention:
            xn4 = sb(attention, "xn4", [P, 4, D])
            xT = [sb(attention, f"xT_{n}", [P, KD, BT], f32r) for n in ("hi", "lo")]
            q = [sb(attention, f"q_{n}", [P, 2, G, BT], f32r) for n in ("hi", "lo")]
            k = [sb(attention, f"k_{n}", [P, 2, BT], f32r) for n in ("hi", "lo")]
            v = [sb(attention, f"v_{n}", [P, 4, KV * DH], f32r) for n in ("hi", "lo")]
            probs = sb(attention, "probs", [P, 2, 4, S])
            probsT = [sb(attention, f"probsT_{n}", [P, 2, 2, S], f32r) for n in ("hi", "lo")]
            o = [sb(attention, f"o_{n}", [P, 2, 2, S], f32r) for n in ("hi", "lo")]
            yT = sb(attention, "yT", [P, KD, BT])
            negmax = sb(attention, "negmax", [P, 2, 4])
            rowsum = sb(attention, "rowsum", [P, 2, 4])
            rowinv = sb(attention, "rowinv", [P, 2, 4])

        bank = [ctx.enter_context(nc.psum_tensor(f"bank{n}", [P, 512], f32)) for n in range(8)]
        scores_ps, probsT_ps, work_ps, out_ps = bank[0:2], bank[2:4], bank[4:6], bank[6:8]

        x_loaded = [sem(f"x_loaded{n}") for n in range(4)]
        small_loaded = sem("small_loaded")
        piece_loaded = sem("piece_loaded")
        piece_high = sem("piece_high")
        weights_split = sem("weights_split")
        bq_scaled = sem("bq_scaled")
        constants = sem("constants")
        key_raw = sem("key_raw")
        key_ready = sem("key_ready")
        setup_link = sem("setup_link")
        link = sem("dve_link")
        zero_stored = sem("zero_stored")
        var_ready = sem("var_ready")
        root_ready = sem("root_ready")
        xn_ready = sem("xn_ready")
        xnT_raw = sem("xnT_raw")
        xnT_ready = sem("xnT_ready")
        logits_raw = sem("logits_raw")
        logits_ready = sem("logits_ready")
        top8_ready = sem("top8_ready")
        shifted = sem("shifted")
        exps = sem("exps")
        chosen_ready = sem("chosen_ready")
        masked = sem("masked")
        winv_ready = sem("winv_ready")
        weights_ready = sem("weights_ready")
        chosenT_raw = sem("chosenT_raw")
        first_ready = sem("first_ready")
        slot_raw = sem("slot_raw")
        slot_ready = sem("slot_ready")
        table_written = sem("table_written")
        gathered = [sem(f"gathered{n}") for n in range(4)]
        up_loaded = [sem(f"up_loaded{n}") for n in range(4)]
        down_loaded = [sem(f"down_loaded{n}") for n in range(2)]
        slotsT_raw = sem("slotsT_raw")
        slotsT_ready = sem("slotsT_ready")
        up_done = sem("up_done")
        gate_ready = sem("gate_ready")
        hidden_ready = sem("hidden_ready")
        hiddenT_raw = sem("hiddenT_raw")
        hiddenT_ready = sem("hiddenT_ready")
        down_done = sem("down_done")
        weight_ready = sem("weight_ready")
        y_high = sem("y_high")
        down_free = sem("down_free")
        onehot_ready = sem("onehot_ready")
        combined = sem("combined")
        x_final = sem("x_final")
        out_stored = sem("out_stored")
        xn4_ready = sem("xn4_ready")
        work_ready = sem("work_ready")
        work_high = sem("work_high")
        work_taken = sem("work_taken")
        scores_ready = sem("scores_ready")
        negmax_ready = sem("negmax_ready")
        exp_ready = sem("exp_ready")
        probs_ready = sem("probs_ready")
        probsT_raw = sem("probsT_raw")
        probsT_high = sem("probsT_high")
        probsT_taken = sem("probsT_taken")
        y_raw = sem("y_raw")
        yT_ready = sem("yT_ready")
        y_ready = sem("y_ready")
        attention_done = sem("attention_done")

        def place(n):
            return n // 4 % KV, n % 4 // 2, n % 2

        first_fills = ([("xT", h, 0) for h in range(KD)] + [("v", t, 0) for t in range(2)] + [("k", 0, 0)]
                       + [("q", g, 0) for g in range(G)])

        def fills(n, last):
            if last and n >= 12:
                return []
            kv = (n // 4 + 1) % KV
            r = n % 4
            more = [("k", 0, kv), ("q", 0, kv)] if r == 0 else [("q", r, kv)]
            if n == 11 and not last:
                more += [("xT", h, 0) for h in range(KD)]
            tile = {14: 0, 15: 1, 0: 2, 16: 2, 1: 3}.get(n)
            if tile is not None:
                more.append(("v", tile, 0))
            return more

        block = ctx.enter_context(nc.Block())

        @block.sync
        def _(sp):
            for n in range(4):
                sp.dma_start(x[:, 4 * n:4 * n + 4, :],
                             x_in[512 * n:512 * n + 512, :].rearrange("(a p) d -> p a d", p=P)).then_inc(x_loaded[n], 16)
            for dst, src in ((router_w, router_in), (bq, bq_in), (bk, bk_in), (bv, bv_in), (bo, bo_in)):
                sp.dma_start(dst[:], src).then_inc(small_loaded, 16)

            xn_seen, weights_seen = Tally(xn_ready), Tally(weights_ready)
            ups_seen, downs_seen = Tally(up_done), Tally(down_done)

            def load_up(g, slot):
                sp.dma_start(up_w[:, slot, :, :, :], up_in[ds(g * P, P), :].rearrange(
                    "p (j k f) -> p j k f", j=EG, k=KD)).then_inc(up_loaded[slot], 16)

            def load_down(g, slot):
                sp.dma_start(down_w[:, slot, :, :], down_in[ds(g * F, F), :].rearrange(
                    "f (j d) -> f j d", j=EG)).then_inc(down_loaded[slot], 16)

            def expert_layer():
                for g in range(4):
                    load_up(g, g)
                for g in range(2):
                    load_down(g, g)
                rows = table[0:T, :].rearrange("(h p b) e -> h p b e", h=2, p=P)
                for n in range(4):
                    sp.wait_ge(xn_ready, xn_seen.add(4))
                    for half in range(2):
                        sp.dma_start(rows[half, :, 2 * n:2 * n + 2, 0:D],
                                     xn[:, 4 * n + half:4 * n + half + 3:2, :]).then_inc(table_written, 16)
                sp.wait_ge(weights_ready, weights_seen.add())
                for half in range(2):
                    sp.dma_start(rows[half, :, :, D:ROW],
                                 expw[:, half:TILES:2, :]).then_inc(table_written, 16)
                with turns(sp, 3, [(ups_seen, 4), (downs_seen, 4)]) as i:
                    for u in range(4):
                        sp.wait_ge(up_done, ups_seen.add())
                        load_up(i * 4 + u + 4, u)
                        sp.wait_ge(down_done, downs_seen.add())
                        load_down(i * 4 + u + 2, u % 2)
                ups_seen.add(4)
                for u in range(2):
                    sp.wait_ge(down_done, downs_seen.add())
                    load_down(14 + u, u)
                downs_seen.add(2)

            expert_layer()
            sp.wait_ge(attention_done, 1)
            expert_layer()
            final_seen = Tally(x_final)
            final_seen.add(TILES)
            with turns(sp, TILES // 2, [(final_seen, 2)]) as i:
                for u in range(2):
                    sp.wait_ge(x_final, final_seen.add())
                    sp.dma_start(out[ds(i * 2 * P + u * P, P), :],
                                 x[:, ds(i * 2 + u, 1), :].rearrange("p a d -> p (a d)")).then_inc(out_stored, 16)
            sp.wait_ge(out_stored, 16 * TILES)

        @block.gpsimd
        def _(pool):
            nc.gpsimd.memset(ident[:], 0.0).then_inc(setup_link, 1)
            nc.gpsimd.iota(token_i32[:], pattern=[[8, 2 * P]], base=0, channel_multiplier=0).then_inc(setup_link, 1)
            nc.gpsimd.memset(zero_row[:], 0.0).then_inc(setup_link, 1)
            pool.wait_ge(setup_link, 3)
            nc.gpsimd.affine_select(out=ident[:], in_=ident[:], compare_op=ALU.not_equal, fill=1.0, base=0,
                                    pattern=[[-1, P]], channel_multiplier=1).then_inc(constants, 1)
            nc.gpsimd.tensor_copy(token_of_column[:].rearrange("p u r -> p (u r)"), token_i32[:]).then_inc(constants, 1)
            pool.wait_ge(constants, 2)
            pool.dma_start(table[T:T + 1, :], zero_row[0:1, :]).then_inc(zero_stored, 16)

            raw, tops, exp_seen = Tally(key_raw), Tally(top8_ready), Tally(exps)
            masks, inv, slot_seen = Tally(chosen_ready), Tally(winv_ready), Tally(slot_ready)
            written = Tally(table_written)
            arrived = [Tally(s) for s in gathered]

            def expert_layer():
                for half in range(2):
                    nc.gpsimd.iota(key_i32[64 * half:64 * half + 64, :], pattern=[[-1, 4], [-1024, 2], [-8, P]],
                                    base=T - 4 * half, channel_multiplier=0).then_inc(key_raw, 1)
                    pool.wait_ge(key_raw, raw.add())
                nc.gpsimd.tensor_copy(key_of_column[:], key_i32[:]).then_inc(key_ready, 1)
                pool.wait_ge(top8_ready, tops.add())
                nc.gpsimd.tensor_tensor(expw[:], logits[:], top8[:, :, 0:1].to_broadcast([P, TILES, E]),
                                        ALU.subtract).then_inc(shifted, 1)
                pool.wait_ge(chosen_ready, masks.add())
                pool.wait_ge(exps, exp_seen.add())
                nc.gpsimd.tensor_tensor(
                    expw[:].rearrange("p (h i) e -> p h i e", h=2), expw[:].rearrange("p (h i) e -> p h i e", h=2),
                    chosen[:].rearrange("p i h e -> p h i e"), ALU.mult).then_inc(masked, 1)
                pool.wait_ge(winv_ready, inv.add())
                nc.gpsimd.tensor_tensor(expw[:], expw[:], wsum[:, 1, :].unsqueeze(2).to_broadcast([P, TILES, E]),
                                        ALU.mult).then_inc(weights_ready, 1)
                pool.wait_ge(slot_ready, slot_seen.add(2))
                pool.wait_ge(table_written, written.add(160))
                pool.wait_ge(zero_stored, 16)
                for g in range(GROUPS):
                    if g >= 4:
                        pool.wait_ge(gathered[g % 4], arrived[g % 4].now())
                    nc.gpsimd.indirect_dma_start(
                        out=slots[:, g, :], out_offset=None, in_=table[:, :],
                        in_offset=bass.IndirectOffsetOnAxis(ap=slot_index[:, g:g + 1], axis=0),
                    ).then_inc(gathered[g % 4], 16)
                    arrived[g % 4].add(16)

            expert_layer()
            half_wo = H // 2
            jobs = [[(piece[:], wq_in[kd * P:kd * P + P, :], [w[:, kd, :] for w in wq], SCALE)] for kd in range(KD)]
            jobs += [[(piece[:, 1024 * n:1024 * n + 1024].rearrange("p (k n) -> p k n", k=KD),
                       src.rearrange("(k p) n -> p k n", p=P), [w[:] for w in parts], None)
                      for n, (src, parts) in enumerate(((wk_in, wk), (wv_in, wv)))]]
            jobs += [[(piece[:].rearrange("p (h d) -> p h d", d=D),
                       wo_in[n * half_wo * DH:(n + 1) * half_wo * DH, :].rearrange("(h p) d -> p h d", p=P),
                       [w[:, n * half_wo:(n + 1) * half_wo, :] for w in wo], None)] for n in range(2)]
            loads, scaled, parts_done = Tally(piece_loaded), Tally(setup_link), 0
            scaled.add(3)
            for job in jobs:
                if parts_done:
                    pool.wait_ge(weights_split, parts_done)
                for dst, src, _, _ in job:
                    pool.dma_start(dst, src).then_inc(piece_loaded, 16)
                    loads.add(16)
                pool.wait_ge(piece_loaded, loads.now())
                for whole, _, _, scale in job:
                    if scale is not None:
                        nc.gpsimd.tensor_scalar(whole, whole, scale, None, ALU.mult).then_inc(setup_link, 1)
                        pool.wait_ge(setup_link, scaled.add())
                for whole, _, (hi, lo), _ in job:
                    nc.gpsimd.tensor_copy(hi, whole).then_inc(piece_high, 1)
                pool.wait_ge(piece_high, parts_done + len(job))
                for whole, _, (hi, lo), _ in job:
                    nc.gpsimd.tensor_tensor(lo, whole, hi.bitcast(f32), ALU.subtract).then_inc(weights_split, 1)
                parts_done += len(job)
            pool.wait_ge(attention_done, 1)
            expert_layer()

        @block.scalar
        def _(act):
            xnT_seen, logits_seen, shift_seen = Tally(xnT_raw), Tally(logits_raw), Tally(shifted)
            sT_seen, up_seen, hT_seen, down_seen = Tally(slotsT_raw), Tally(up_done), Tally(hiddenT_raw), Tally(down_done)
            weight_seen, vars_seen = Tally(weight_ready), Tally(var_ready)

            def deviations():
                act.wait_ge(var_ready, vars_seen.add())
                nc.scalar.activation(ln[:, 3, :], ln[:, 4, :], ACT.Sqrt).then_inc(root_ready, 1)

            def slot_step(s, parity, nxt, cur, prev):
                if prev:
                    act.wait_ge(hiddenT_raw, hT_seen.add())
                    nc.scalar.copy(hiddenT[:, 1 - parity, :], bank[5 - parity][0:F, 0:P]).then_inc(hiddenT_ready, 1)
                if nxt:
                    act.wait_ge(slotsT_raw, sT_seen.add())
                    nc.scalar.copy(slotsT[:, 1 - parity, :, :].rearrange("p k t -> p (k t)"),
                                   bank[1 - parity][:, 0:KD * P]).then_inc(slotsT_ready, 1)
                if cur:
                    act.wait_ge(up_done, up_seen.add())
                    nc.scalar.activation(gate[:, parity, :], bank[2 + parity][:, 0:F], ACT.Silu).then_inc(gate_ready, 1)
                if prev:
                    act.wait_ge(weight_ready, weight_seen.add())
                    act.wait_ge(down_done, down_seen.add())
                    nc.scalar.activation(y_parts[:, ds(s - 1, 1), 0, :].rearrange("p a d -> p (a d)"), bank[7 - parity][:, 0:D],
                                         ACT.Identity, scale=slot_weight[:, ds(s - 1, 1)]).then_inc(y_high, 1)

            def expert_layer():
                deviations()
                with turns(nc.scalar, 4, [(xnT_seen, 2), (logits_seen, 1)]) as i:
                    for pair in range(2):
                        act.wait_ge(xnT_raw, xnT_seen.add())
                        nc.scalar.copy(xnT[:, pair].rearrange("p t k c -> p (t k c)"), bank[pair][:]).then_inc(xnT_ready, 1)
                    act.wait_ge(logits_raw, logits_seen.add())
                    nc.scalar.copy(logits[:, ds(i * 4, 4), :].rearrange("p t e -> p (t e)"),
                                   bank[2][:, 0:4 * E]).then_inc(logits_ready, 1)
                act.wait_ge(shifted, shift_seen.add())
                nc.scalar.activation(expw[:], expw[:], ACT.Exp).then_inc(exps, 1)
                act.wait_ge(slotsT_raw, sT_seen.add())
                nc.scalar.copy(slotsT[:, 0, :, :].rearrange("p k t -> p (k t)"), bank[0][:, 0:KD * P]).then_inc(slotsT_ready, 1)
                slot_step(0, 0, True, True, False)
                with turns(nc.scalar, 3, [(hT_seen, 4), (sT_seen, 4), (up_seen, 4), (weight_seen, 4), (down_seen, 4)]) as i:
                    for u in range(4):
                        slot_step(i * 4 + 1 + u, (1 + u) % 2, True, True, True)
                for s in range(13, GROUPS + 1):
                    slot_step(s, s % 2, s < GROUPS - 1, s < GROUPS, True)

            expert_layer()

            work_seen, pT_seen = Tally(work_ready), Tally(probsT_raw)
            scores_seen, max_seen, y_seen = Tally(scores_ready), Tally(negmax_ready), Tally(y_raw)
            uses = [0]

            def take_high(dst, bias=None):
                act.wait_ge(work_ready, work_seen.add())
                src = work_ps[uses[0] % 2]
                uses[0] += 1
                src = src[:] if dst.ndim == 2 else src[:].rearrange("p (h s) -> p h s", h=2)
                if bias is None:
                    nc.scalar.copy(dst, src).then_inc(work_high, 1)
                else:
                    nc.scalar.activation(dst, src, ACT.Identity, bias=bias).then_inc(work_high, 1)

            def take_fill(what, n, kv):
                if what == "k":
                    take_high(k[0][:, kv % 2, :], bk[:, kv:kv + 1])
                elif what == "q":
                    take_high(q[0][:, kv % 2, n, :], bq[:, G * kv + n:G * kv + n + 1])
                else:
                    take_high((xT if what == "xT" else v)[0][:, n, :])

            def exps_of(n, head):
                act.wait_ge(scores_ready, scores_seen.add())
                act.wait_ge(negmax_ready, max_seen.add())
                for qt in range(2):
                    t = 2 * head + qt
                    nc.scalar.activation(probs[:, n % 2, t, :], scores_ps[head][:, qt * S:qt * S + S], ACT.Exp,
                                         bias=negmax[:, n % 2, t:t + 1],
                                         accum_out=rowsum[:, n % 2, t:t + 1]).then_inc(exp_ready, 1)

            def output():
                act.wait_ge(y_raw, y_seen.add())
                for d in range(KD):
                    nc.scalar.activation(yT[:, d, :], out_ps[d][:], ACT.Identity, bias=bo[:, d:d + 1]).then_inc(yT_ready, 1)

            def step(n, last=False):
                kv, bb, hp = place(n)
                for head in range(2):
                    act.wait_ge(probsT_raw, pT_seen.add())
                    nc.scalar.copy(probsT[0][:, head].rearrange("p c s -> p (c s)"),
                                   probsT_ps[head][:]).then_inc(probsT_high, 1)
                jobs = fills(n, last)
                for head in range(2):
                    if not (last and n == 15):
                        exps_of(n + 1, head)
                    if head == 0 and jobs:
                        take_fill(*jobs.pop(0))
                if n == STEPS:
                    output()
                for job in jobs:
                    take_fill(*job)
                take_high(o[0][:, n % 2, :, :], bv[:, kv:kv + 1])
                if n == STEPS:
                    uses[0] += 2

            act.wait_ge(small_loaded, 80)
            act.wait_ge(bq_scaled, 1)
            deviations()
            for job in first_fills:
                take_fill(*job)
            for head in range(2):
                exps_of(0, head)
            step(0)
            with turns(nc.scalar, BLOCKS - 1, [(work_seen, WORK_PER_BLOCK - 2), (pT_seen, 32), (scores_seen, 32),
                                               (max_seen, 32), (y_seen, 1)]):
                for n in range(1, STEPS + 1):
                    step(n)
            for n in range(1, STEPS):
                step(n, last=True)
            output()
            expert_layer()

        @block.vector
        def _(dve):
            linked = Tally(link)

            def tie(ins):
                ins.then_inc(link, 1)
                dve.wait_ge(link, linked.add())

            nc.vector.sem_inc(down_free, 2)
            tie(nc.vector.memset(quadrant[:], 0.0))
            for j in range(EG):
                last = nc.vector.memset(quadrant[32 * j:32 * j + 32, j:j + 1], 1.0)
            tie(last)
            logits_seen, key_seen, pairs_seen = Tally(logits_ready), Tally(key_ready), Tally(chosenT_raw)
            masked_seen, slot_seen, gates_seen = Tally(masked), Tally(slot_raw), Tally(gate_ready)
            high_seen, combined_seen = Tally(y_high), Tally(combined)
            arrived = [Tally(s) for s in gathered]
            roots_seen = Tally(root_ready)

            def layer_norm_stats(first):
                for a in range(TILES):
                    if first and a % 4 == 0:
                        dve.wait_ge(x_loaded[a // 4], 16)
                    last = nc.vector.bn_stats(stats[:, a, :], x[:, a, :])
                tie(last)
                even, odd = stats[:, :, 1], stats[:, :, 4]
                half_gap, gap2, var = ln[:, 2, :], ln[:, 3, :], ln[:, 4, :]
                nc.vector.tensor_tensor(mean, even, odd, ALU.add)
                nc.vector.tensor_tensor(var, stats[:, :, 2], stats[:, :, 5], ALU.add)
                tie(nc.vector.tensor_tensor(half_gap, even, odd, ALU.subtract))
                tie(nc.vector.scalar_tensor_tensor(gap2, half_gap, 0.25, half_gap, ALU.mult, ALU.mult))
                nc.vector.tensor_scalar(mean, mean, 0.5, None, ALU.mult)
                tie(nc.vector.scalar_tensor_tensor(var, var, 1.0 / D, gap2, ALU.mult, ALU.add))
                nc.vector.tensor_scalar(var, var, EPS, None, ALU.add).then_inc(var_ready, 1)
                dve.wait_ge(root_ready, roots_seen.add())
                tie(nc.vector.reciprocal(rstd, gap2))
                tie(nc.vector.tensor_tensor(gap2, rstd, rstd, ALU.mult))
                tie(nc.vector.tensor_tensor(gap2, gap2, var, ALU.mult))
                tie(nc.vector.tensor_scalar(gap2, gap2, -0.5, 1.5, ALU.mult, ALU.add))
                tie(nc.vector.tensor_tensor(rstd, rstd, gap2, ALU.mult))

            def slot_step(s, parity, u, cur, prev):
                if cur:
                    dve.wait_ge(gathered[u], arrived[u].add(16))
                    tie(nc.vector.tensor_tensor(weight4[:, parity, :], slots[:, ds(s, 1), ds(s + D, EG, step=GROUPS)].rearrange(
                        "p a e -> p (a e)"), quadrant[:], ALU.mult))
                    nc.vector.tensor_reduce(slot_weight[:, ds(s, 1)], weight4[:, parity, :], AX.X, ALU.add).then_inc(weight_ready, 1)
                    dve.wait_ge(gate_ready, gates_seen.add())
                    nc.vector.tensor_tensor(hidden[:, parity, :], gate[:, parity, :], bank[2 + parity][:, F:2 * F],
                                            ALU.mult).then_inc(hidden_ready, 1)
                if prev:
                    dve.wait_ge(y_high, high_seen.add())
                    nc.vector.scalar_tensor_tensor(
                        y_parts[:, ds(s - 1, 1), 1, :].rearrange("p a d -> p (a d)"), bank[7 - parity][:, 0:D],
                        slot_weight[:, ds(s - 1, 1)],
                        y_parts[:, ds(s - 1, 1), 0, :].rearrange("p a d -> p (a d)").bitcast(f32),
                        ALU.mult, ALU.subtract).then_inc(down_free, 1)

            def expert_layer(first):
                layer_norm_stats(first)
                for a in range(TILES):
                    nc.vector.tensor_scalar(xn[:, a, :], x[:, a, :], mean[:, a:a + 1], rstd[:, a:a + 1],
                                            ALU.subtract, ALU.mult).then_inc(xn_ready, 1)
                for a in range(TILES):
                    if a % 4 == 0:
                        dve.wait_ge(logits_ready, logits_seen.add())
                    last = nc.vector.max(top8[:, a, :], logits[:, a, :])
                last.then_inc(top8_ready, 1)
                dve.wait_ge(top8_ready, 1 if first else 2)
                for a in range(TILES):
                    last = nc.vector.match_replace(struck[:, a, :], top8[:, a, :], logits[:, a, :], LOWEST)
                tie(last)
                nc.vector.tensor_scalar(chosen[:].rearrange("p i h e -> p h i e"),
                                        struck[:].rearrange("p (h i) e -> p h i e", h=2), 0.99 * LOWEST, None,
                                        ALU.is_lt).then_inc(chosen_ready, 1)
                dve.wait_ge(key_ready, key_seen.add())
                for n in range(2):
                    dve.wait_ge(chosenT_raw, pairs_seen.add())
                    last = nc.vector.tensor_tensor(keys[:, 512 * n:512 * n + 512], bank[n][:],
                                                   key_of_column[:, 512 * n:512 * n + 512], ALU.mult)
                tie(last)
                for n in range(C // 8):
                    tie(nc.vector.max(best[:, 8 * n:8 * n + 8], keys[:]))
                    if n < C // 8 - 1:
                        tie(nc.vector.match_replace(keys[:], best[:, 8 * n:8 * n + 8], keys[:], -1.0))
                    if n == 1:
                        dve.wait_ge(masked, masked_seen.add())
                        tie(nc.vector.tensor_reduce(wsum[:, 0, :], expw[:], AX.X, ALU.add))
                        tie(nc.vector.reciprocal(wsum[:, 1, :], wsum[:, 0, :]))
                        nc.vector.tensor_scalar(wsum[:, 1, :], wsum[:, 1, :], 0.5, None, ALU.mult).then_inc(winv_ready, 1)
                nc.vector.tensor_copy(merged[:, 0:C], best[0:E, :])
                tie(nc.vector.tensor_copy(merged[:, C:2 * C], best[E:P, :]))
                for n in range(C // 8):
                    last = nc.vector.max(first_keys(n), merged[:])
                    if n < C // 8 - 1:
                        tie(last)
                        tie(nc.vector.match_replace(merged[:], first_keys(n), merged[:], -1.0))
                last.then_inc(first_ready, 1)
                dve.wait_ge(slot_raw, slot_seen.add())
                for dst in (slot_token, slot_index):
                    nc.vector.tensor_scalar(dst[:], bank[4][:, 0:GROUPS], -1.0, float(T), ALU.mult, ALU.add).then_inc(slot_ready, 1)

                slot_step(0, 0, 0, True, False)
                with turns(nc.vector, 3, [(linked, 4), (gates_seen, 4), (high_seen, 4)] + [(t, 16) for t in arrived]) as i:
                    for u in range(4):
                        slot_step(i * 4 + 1 + u, (1 + u) % 2, (1 + u) % 4, True, True)
                for s in range(13, GROUPS + 1):
                    slot_step(s, s % 2, s % 4, s < GROUPS, True)

                dve.wait_ge(slot_ready, 2 if first else 4)

                def mark(u):
                    nc.vector.tensor_tensor(onehot[:, u, :, :], token_of_column[:, u:u + 1, :].to_broadcast([P, GROUPS, P]),
                                            slot_token[:].unsqueeze(2).to_broadcast([P, GROUPS, P]),
                                            ALU.is_equal).then_inc(onehot_ready, 1)

                def add(a, u):
                    dve.wait_ge(combined, combined_seen.add())
                    xa = x[:, ds(a, 1), :].rearrange("p a d -> p (a d)")
                    tie(nc.vector.tensor_tensor(xa, xa, bank[u][:, 0:D], ALU.add))
                    nc.vector.tensor_tensor(xa, xa, bank[u][:, D:2 * D], ALU.add).then_inc(x_final, 1)

                mark(0)
                with turns(nc.vector, TILES // 2 - 1, [(linked, 3), (combined_seen, 2)]) as i:
                    mark(1)
                    add(i * 2, 0)
                    tie(nc.vector.tensor_scalar(slot_token[:], slot_token[:], -1.0, None, ALU.add))
                    mark(0)
                    add(i * 2 + 1, 1)
                mark(1)
                add(TILES - 2, 0)
                add(TILES - 1, 1)
                dve.wait_ge(x_final, TILES if first else 2 * TILES)

            def first_keys(n):
                return slot_keys[:, 8 * n:8 * n + 8]

            expert_layer(True)
            dve.wait_ge(small_loaded, 80)
            nc.vector.tensor_scalar(bq[:], bq[:], SCALE, None, ALU.mult).then_inc(bq_scaled, 1)
            dve.wait_ge(bq_scaled, 1)

            high_work, pT_high = Tally(work_high), Tally(probsT_high)
            scores_seen, exp_seen, y_seen = Tally(scores_ready), Tally(exp_ready), Tally(y_ready)
            uses = [0]

            def normalise_tokens(i):
                for t in range(4):
                    a = i * 4 + t if isinstance(i, int) else i * 4 + (t + 4)
                    last = nc.vector.tensor_scalar(xn4[:, t, :], x[:, ds(a, 1), :].rearrange("p a d -> p (a d)"),
                                                   mean[:, ds(a, 1)], rstd[:, ds(a, 1)], ALU.subtract, ALU.mult)
                last.then_inc(xn4_ready, 1)

            def take_low(hi, lo, bias=None):
                dve.wait_ge(work_high, high_work.add())
                src = work_ps[uses[0] % 2]
                uses[0] += 1
                src = src[:] if hi.ndim == 2 else src[:].rearrange("p (h s) -> p h s", h=2)
                if bias is None:
                    nc.vector.tensor_tensor(lo, src, hi.bitcast(f32), ALU.subtract).then_inc(work_taken, 1)
                else:
                    nc.vector.scalar_tensor_tensor(lo, src, bias, hi.bitcast(f32), ALU.add, ALU.subtract).then_inc(work_taken, 1)

            def take_fill(what, n, kv):
                if what == "k":
                    take_low(*[t[:, kv % 2, :] for t in k], bk[:, kv:kv + 1])
                elif what == "q":
                    take_low(*[t[:, kv % 2, n, :] for t in q], bq[:, G * kv + n:G * kv + n + 1])
                else:
                    take_low(*[t[:, n, :] for t in (xT if what == "xT" else v)])

            def maxima(n):
                for head in range(2):
                    dve.wait_ge(scores_ready, scores_seen.add())
                    nc.vector.reduce_max(negmax[:, n % 2, 2 * head:2 * head + 2],
                                         scores_ps[head][:].rearrange("p (t s) -> p t s", t=2), AX.X,
                                         negate=True).then_inc(negmax_ready, 1)

            def normalise_probs(n):
                dve.wait_ge(exp_ready, exp_seen.add(4))
                tie(nc.vector.reciprocal(rowinv[:, n % 2, :], rowsum[:, n % 2, :]))
                for t in range(4):
                    last = nc.vector.tensor_scalar(probs[:, n % 2, t, :], probs[:, n % 2, t, :],
                                                   rowinv[:, n % 2, t:t + 1], None, ALU.mult)
                last.then_inc(probs_ready, 1)

            def output(i):
                for pair in range(2):
                    dve.wait_ge(y_ready, y_seen.add())
                    xa = x[:, ds(i * 4 + 2 * pair, 2), :].rearrange("p t d -> p (t d)")
                    nc.vector.tensor_tensor(xa, xa, work_ps[uses[0] % 2][:], ALU.add).then_inc(work_taken, 1)
                    uses[0] += 1

            def step(n, i=None, last=False):
                kv, bb, hp = place(n)
                if not (last and n == 15):
                    maxima(n + 1)
                for head in range(2):
                    dve.wait_ge(probsT_high, pT_high.add())
                    nc.vector.tensor_tensor(probsT[1][:, head].rearrange("p c s -> p (c s)"), probsT_ps[head][:],
                                            probsT[0][:, head].rearrange("p c s -> p (c s)").bitcast(f32),
                                            ALU.subtract).then_inc(probsT_taken, 1)
                jobs = fills(n, last)
                if jobs:
                    take_fill(*jobs.pop(0))
                if not (last and n == 15):
                    normalise_probs(n + 1)
                for job in jobs:
                    take_fill(*job)
                if n == 9 and not last:
                    normalise_tokens(i)
                take_low(*[t[:, n % 2, :, :] for t in o], bv[:, kv:kv + 1])
                if n == STEPS:
                    output(i)

            layer_norm_stats(False)
            dve.wait_ge(weights_split, SPLITS)
            normalise_tokens(0)
            for job in first_fills:
                take_fill(*job)
            maxima(0)
            normalise_probs(0)
            step(0)
            with turns(nc.vector, BLOCKS - 1, [(linked, 16), (high_work, WORK_PER_BLOCK - 2), (pT_high, 32),
                                               (scores_seen, 32), (exp_seen, 64), (y_seen, 2)]) as i:
                for n in range(1, STEPS + 1):
                    step(n, i)
            for n in range(1, STEPS):
                step(n, last=True)
            output(BLOCKS - 1)
            dve.wait_ge(work_taken, len(first_fills) + BLOCKS * WORK_PER_BLOCK - (1 + G) - KD - 2)
            nc.vector.sem_inc(attention_done, 1)
            expert_layer(False)

        @block.tensor
        def _(pe):
            mm = nc.tensor.matmul
            xn_seen, xnT_seen, logits_taken = Tally(xn_ready), Tally(xnT_ready), Tally(logits_ready)
            chosen_seen, keys_seen = Tally(chosen_ready), Tally(first_ready)
            arrived = [Tally(s) for s in gathered]
            up_in_seen, down_in_seen = [Tally(s) for s in up_loaded], [Tally(s) for s in down_loaded]
            sT_seen, hidden_seen, hT_seen = Tally(slotsT_ready), Tally(hidden_ready), Tally(hiddenT_ready)
            free_seen, hot_seen = Tally(down_free), Tally(onehot_ready)

            def transpose_slots(s, parity, u):
                pe.wait_ge(gathered[u], arrived[u].add(16))
                for kd in range(KD):
                    last = nc.tensor.transpose(bank[parity][:, kd * P:kd * P + P],
                                               slots[:, s, kd * P:kd * P + P], ident[:])
                last.then_inc(slotsT_raw, 1)

            def slot_step(s, parity, nxt, cur, prev):
                if prev:
                    pe.wait_ge(hidden_ready, hidden_seen.add())
                    nc.tensor.transpose(bank[5 - parity][0:F, 0:P], hidden[:, 1 - parity, :], ident[:]).then_inc(hiddenT_raw, 1)
                if nxt:
                    transpose_slots(s + 1, 1 - parity, (s + 1) % 4)
                if cur:
                    pe.wait_ge(slotsT_ready, sT_seen.add())
                    pe.wait_ge(up_loaded[s % 4], up_in_seen[s % 4].add(16))
                    for kd in range(KD):
                        for j in range(EG):
                            last = mm(bank[2 + parity][32 * j:32 * j + 32, 0:2 * F], slotsT[:, parity, kd, 32 * j:32 * j + 32],
                                      up_w[:, s % 4, j, kd, :], start=kd == 0, stop=kd == KD - 1, tile_position=(0, 32 * j))
                    last.then_inc(up_done, 1)
                if prev:
                    pe.wait_ge(hiddenT_ready, hT_seen.add())
                    pe.wait_ge(down_loaded[1 - parity], down_in_seen[1 - parity].add(16))
                    pe.wait_ge(down_free, free_seen.add())
                    for j in range(EG):
                        last = mm(bank[7 - parity][32 * j:32 * j + 32, 0:D], hiddenT[:, 1 - parity, 32 * j:32 * j + 32],
                                  down_w[:, 1 - parity, j, :], start=True, stop=True, tile_position=(0, 32 * j))
                    last.then_inc(down_done, 1)

            def expert_layer(first):
                for n in range(4):
                    for pair in range(2):
                        pe.wait_ge(xn_ready, xn_seen.add(2))
                        for t in range(2):
                            for kd in range(KD):
                                c = (2 * t + kd) * P
                                last = nc.tensor.transpose(bank[pair][:, c:c + P],
                                                           xn[:, 4 * n + 2 * pair + t, kd * P:kd * P + P], ident[:])
                        last.then_inc(xnT_raw, 1)
                    for pair in range(2):
                        pe.wait_ge(xnT_ready, xnT_seen.add())
                        if pair == 0 and logits_taken.now() > 0:
                            pe.wait_ge(logits_ready, logits_taken.now())
                        for t in range(2):
                            for kd in range(KD):
                                last = mm(bank[2][:, (2 * pair + t) * E:(2 * pair + t + 1) * E], xnT[:, pair, t, kd, :],
                                          router_w[:, kd, :], start=kd == 0, stop=kd == KD - 1)
                    last.then_inc(logits_raw, 1)
                    logits_taken.add()
                pe.wait_ge(chosen_ready, chosen_seen.add())
                for n in range(2):
                    for c in range(4):
                        last = nc.tensor.transpose(bank[n][:, c * P:c * P + P],
                                                   chosen[:, 4 * n + c, :, :].rearrange("p h e -> p (h e)"), ident[:])
                    last.then_inc(chosenT_raw, 1)
                pe.wait_ge(first_ready, keys_seen.add())
                for j in range(EG):
                    last = mm(bank[4][32 * j:32 * j + 32, 0:GROUPS], slot_keys[:], ident[0:E, GROUPS * j:GROUPS * j + GROUPS],
                              start=True, stop=True, tile_position=(0, 32 * j))
                last.then_inc(slot_raw, 1)
                transpose_slots(0, 0, 0)
                for s in range(GROUPS + 1):
                    slot_step(s, s % 2, s < GROUPS - 1, s < GROUPS, s > 0)
                pe.wait_ge(down_free, free_seen.now() + 2)

                with turns(nc.tensor, TILES // 2, [(hot_seen, 2)]) as i:
                    for u in range(2):
                        pe.wait_ge(onehot_ready, hot_seen.add())
                        for g in range(GROUPS):
                            last = mm(bank[u][:], onehot[:, u, g, :], y_parts[:, g, :, :].rearrange("p a d -> p (a d)"),
                                      start=g == 0, stop=g == GROUPS - 1)
                        last.then_inc(combined, 1)

            pe.wait_ge(constants, 2)
            pe.wait_ge(small_loaded, 80)
            expert_layer(True)

            xn4_seen, pT_taken, probs_seen, yT_seen = Tally(xn4_ready), Tally(probsT_taken), Tally(probs_ready), Tally(yT_ready)
            exp_seen, scored, uses = Tally(exp_ready), [False], [0]
            issued = Tally(work_taken)
            last_use = {}

            def work(*needed):
                back = min([1] + [uses[0] - last_use[what] for what in needed])
                if issued.turn is not None or issued.fixed > back:
                    pe.wait_ge(work_taken, issued.now(back=back))
                issued.add()
                uses[0] += 1
                return work_ps[(uses[0] - 1) % 2]

            def three(dst, w, m, start, stop, shared=False):
                mm(dst, w[0], m[0], start=start, stop=False, skip_group_check=shared)
                mm(dst, w[0], m[1], start=False, stop=False, skip_group_check=shared)
                return mm(dst, w[1], m[0], start=False, stop=stop, skip_group_check=shared)

            def on_chip(what):
                pe.wait_ge(work_taken, issued.now(back=uses[0] - last_use[what]))

            def project(what, n, kv, *needed):
                ps = work(*needed)
                if what == "xT":
                    for t in range(4):
                        last = nc.tensor.transpose(ps[:, t * P:t * P + P], xn4[:, t, n * P:n * P + P], ident[:])
                elif what == "v":
                    for kd in range(KD):
                        last = three(ps[:], [a[:, kd, n * P:n * P + P] for a in xT], [a[:, kd, :] for a in wv], kd == 0, kd == KD - 1)
                else:
                    w, c = (wk, kv * DH) if what == "k" else (wq, (G * kv + n) * DH)
                    for kd in range(KD):
                        last = three(ps[:], [a[:, kd, c:c + DH] for a in w], [a[:, kd, :] for a in xT], kd == 0, kd == KD - 1)
                last.then_inc(work_ready, 1)
                last_use[(what, n) if what in "qv" else what] = uses[0]

            def scores(n):
                kv, bb, hp = place(n)
                if n % 4 < 2:
                    on_chip(("q", 2 * hp + 1))
                for head in range(2):
                    if scored[0]:
                        pe.wait_ge(exp_ready, exp_seen.add(2))
                    for qt in range(2):
                        c = bb * S + qt * P
                        last = three(scores_ps[head][:, qt * S:qt * S + S], [a[:, kv % 2, 2 * hp + head, c:c + P] for a in q],
                                     [a[:, kv % 2, bb * S:bb * S + S] for a in k], True, True)
                    last.then_inc(scores_ready, 1)
                scored[0] = True

            def transpose_probs(n):
                pe.wait_ge(probs_ready, probs_seen.add())
                for head in range(2):
                    for qt in range(2):
                        for c in range(2):
                            last = nc.tensor.transpose(probsT_ps[head][:, c * S + qt * P:c * S + qt * P + P],
                                                       probs[:, n % 2, 2 * head + qt, c * P:c * P + P], ident[:])
                    last.then_inc(probsT_raw, 1)

            def output_product(n):
                kv, bb, hp = place(n)
                on_chip("o")
                for d in range(KD):
                    for head in range(2):
                        last = three(out_ps[d][:, bb * S:bb * S + S], [a[:, G * kv + 2 * hp + head, d * P:d * P + P] for a in wo],
                                     [a[:, n % 2, head, :] for a in o], n % STEPS == 0 and head == 0, n % STEPS == STEPS - 1 and head == 1,
                                     shared=True)
                if n % STEPS == STEPS - 1:
                    last.then_inc(y_raw, 1)

            def output():
                pe.wait_ge(yT_ready, yT_seen.add(KD))
                for pair in range(2):
                    ps = work()
                    for t in range(2):
                        for d in range(KD):
                            c = (2 * pair + t) * P
                            last = nc.tensor.transpose(ps[:, t * D + d * P:t * D + d * P + P], yT[:, d, c:c + P], ident[:])
                    last.then_inc(y_ready, 1)

            def step(n, last=False):
                kv, bb, hp = place(n)
                if not (last and n == 15):
                    scores(n + 1)
                transpose_probs(n)
                if n == STEPS:
                    output_product(n - 1)
                jobs = fills(n, last)
                for m, job in enumerate(jobs):
                    if n == 11 and job[0] == "xT" and job[1] == 0:
                        pe.wait_ge(xn4_ready, xn4_seen.add())
                    project(*job, *(["xT"] if n == 12 and m == 0 else []))
                    if m == 0 and 0 < n < STEPS:
                        output_product(n - 1)
                if not jobs:
                    output_product(n - 1)
                pe.wait_ge(probsT_taken, pT_taken.add(2))
                ps = work(*([("v", 2 * bb + 1)] if n % STEPS in (0, 2) else []))
                for c in range(2):
                    product = three(ps[:].rearrange("p (h s) -> p h s", h=2), [a[:, 2 * bb + c, kv * DH:kv * DH + DH] for a in v],
                                    [a[:, :, c, :] for a in probsT], c == 0, c == 1)
                product.then_inc(work_ready, 1)
                last_use["o"] = uses[0]
                if n == STEPS:
                    output()

            pe.wait_ge(weights_split, SPLITS)
            pe.wait_ge(xn4_ready, xn4_seen.add())
            for n, job in enumerate(first_fills):
                project(*job, *(["xT"] if n == KD else []))
            scores(0)
            step(0)
            with turns(nc.tensor, BLOCKS - 1, [(issued, WORK_PER_BLOCK), (xn4_seen, 1), (pT_taken, 32), (probs_seen, 16),
                                               (exp_seen, 64), (yT_seen, KD)]):
                for n in range(1, STEPS + 1):
                    step(n)
            for n in range(1, STEPS):
                step(n, last=True)
            output_product(STEPS - 1)
            output()
            expert_layer(False)


def kernel(L0_attn_x, L0_attn_Wq, L0_attn_bq, L0_attn_Wk, L0_attn_bk, L0_attn_Wv, L0_attn_bv, L0_attn_Wo, L0_attn_bo,
           L0_ffn_router_w, L0_ffn_w1, L0_ffn_v1, L0_ffn_w2):
    import concourse.bacc as bacc
    from concourse.bass_utils import run_bass_kernel_spmd

    def arr(a):
        return np.ascontiguousarray(a)

    up = np.concatenate([np.asarray(L0_ffn_w1), np.asarray(L0_ffn_v1)], axis=1)
    up = up.reshape(EG, GROUPS, 2 * F, KD, P).transpose(1, 4, 0, 3, 2).reshape(GROUPS * P, EG * KD * 2 * F)
    down = np.asarray(L0_ffn_w2).reshape(EG, GROUPS, F, D).transpose(1, 2, 0, 3).reshape(GROUPS * F, EG * D)
    arrays = {
        "x_in": arr(np.asarray(L0_attn_x).reshape(T, D)),
        "wq_in": arr(L0_attn_Wq), "bq_in": arr(np.asarray(L0_attn_bq).reshape(H, DH).T),
        "wk_in": arr(L0_attn_Wk), "bk_in": arr(np.asarray(L0_attn_bk).reshape(KV, DH).T),
        "wv_in": arr(L0_attn_Wv), "bv_in": arr(np.asarray(L0_attn_bv).reshape(KV, DH).T),
        "wo_in": arr(L0_attn_Wo), "bo_in": arr(np.asarray(L0_attn_bo).reshape(KD, P).T),
        "router_in": arr(np.asarray(L0_ffn_router_w).reshape(E, KD, P).transpose(2, 1, 0)),
        "up_in": arr(up), "down_in": arr(down),
    }
    nc = bacc.Bacc("TRN2", target_bir_lowering=False, num_devices=1)
    args = [nc.dram_tensor(n, a.shape, mybir.dt.from_np(a.dtype), kind="ExternalInput").ap() for n, a in arrays.items()]
    result = nc.dram_tensor("out", (T, D), mybir.dt.float32, kind="ExternalOutput").ap()
    macaron_kernel(nc, *args, result)
    r = run_bass_kernel_spmd(nc, [arrays], core_ids=[0])
    return r.results[0]["out"].reshape(B, S, D)
```

```python
import concourse.bass as bass
from concourse import mybir
from contextlib import ExitStack, contextmanager
import numpy as np

B, S, D = 8, 256, 256
P = 128
T = B * S
TILES = T // P
KD = D // P
H, DH, KV = 16, 128, 4
G = H // KV
E, F, C = 64, 96, 32
EG = 4
GROUPS = E // EG
ROW = D + E
BLOCKS = 4
BT = T // BLOCKS
EPS = 1e-5
SCALE = 1.0 / float(np.sqrt(DH))
LOWEST = -3.0e38
ROOT_BITS = float(0x5f3759df)
STEPS = 16
WORK_PER_BLOCK = KV * (G + 1) + KD + STEPS + 4 + 2
CHUNK = 256
CHUNKS = T // CHUNK
PARTS = 4
PG = GROUPS // PARTS
SPLITS = KD + 2 + 2


class Tally:

    def __init__(self, sem):
        self.sem, self.fixed, self.turn = sem, 0, None

    def add(self, n=1):
        self.fixed += n
        return self.now()

    def now(self, back=0):
        value = self.fixed - back
        return value if self.turn is None else self.turn + value


@contextmanager
def turns(engine, count, rates):
    with engine.Fori(0, count) as i:
        before = [t.fixed for t, _ in rates]
        for t, per in rates:
            t.turn = i * per
        yield i
        for (t, per), was in zip(rates, before):
            assert t.fixed - was == per, (t.fixed - was, per)
    for t, per in rates:
        t.fixed += per * (count - 1)
        t.turn = None


def macaron_kernel(nc, x_in, wq_in, bq_in, wk_in, bk_in, wv_in, bv_in, wo_in, bo_in, router_in, up_in, down_in, out):
    f32, f32r, i32, u32 = mybir.dt.float32, mybir.dt.float32r, mybir.dt.int32, mybir.dt.uint32
    ALU, ACT, AX = mybir.AluOpType, mybir.ActivationFunctionType, mybir.AxisListType
    ds = bass.ds

    table = nc.dram_tensor("token_table", (T + 1, ROW), f32).ap()

    ctx = ExitStack()
    with ctx:
        def sem(name):
            return ctx.enter_context(nc.semaphore(name))

        def sb(stack, name, shape, dt=f32):
            return stack.enter_context(nc.sbuf_tensor(name, shape, dt))

        x = sb(ctx, "x", [P, TILES, D])
        ident = sb(ctx, "ident", [P, P])
        token_of_column = sb(ctx, "token_of_column", [P, CHUNK])
        token_i32 = sb(ctx, "token_i32", [P, CHUNK], i32)
        quadrant = sb(ctx, "quadrant", [P, EG])
        router_w = sb(ctx, "router_w", [P, KD, E])
        bq = sb(ctx, "bq", [P, H])
        bk = sb(ctx, "bk", [P, KV])
        bv = sb(ctx, "bv", [P, KV])
        bo = sb(ctx, "bo", [P, KD])
        warmed = sb(ctx, "warmed", [P, 1])
        stats = sb(ctx, "stats", [P, TILES, 6])
        ln = sb(ctx, "ln", [P, 6, TILES])
        mean, rstd = ln[:, 0, :], ln[:, 1, :]
        slot_token = sb(ctx, "slot_token", [P, GROUPS])
        slot_index = sb(ctx, "slot_index", [P, GROUPS], u32)
        slot_weight = sb(ctx, "slot_weight", [P, GROUPS])
        held_token = sb(ctx, "held_token", [P, GROUPS])
        last_token = sb(ctx, "last_token", [P, 2])
        limit = sb(ctx, "limit", [1, 1], i32)
        zero_row = sb(ctx, "zero_row", [1, ROW])
        UP, DOWN = EG * KD * 2 * F, EG * D
        def homes(stack, name, count):
            ups, downs = sb(stack, f"up_{name}", [P, count, UP]), sb(stack, f"down_{name}", [F, count, DOWN])
            return [(ups[:, n, :].rearrange("p (j k f) -> p j k f", j=EG, k=KD), downs[:, n, :].rearrange("f (j d) -> f j d", j=EG),
                     sem(f"loaded_{name}{n}")) for n in range(count)]
        with ExitStack() as lent:
            homes_q = homes(lent, "q", 4)
        wq = [sb(ctx, f"wq_{n}", [P, KD, H * DH], f32r) for n in ("hi", "lo")]
        wk = [sb(ctx, f"wk_{n}", [P, KD, KV * DH], f32r) for n in ("hi", "lo")]
        wv = [sb(ctx, f"wv_{n}", [P, KD, KV * DH], f32r) for n in ("hi", "lo")]
        with ExitStack() as lent:
            homes_o = homes(lent, "o", 3)
        wo = [sb(ctx, f"wo_{n}", [P, H, D], f32r) for n in ("hi", "lo")]

        moe = ExitStack()
        with moe:
            with ExitStack() as ring:
                homes_r = homes(ring, "r", 3)
            with ExitStack() as ring:
                onehot = sb(ring, "onehot", [P, PARTS, PG, CHUNK], f32r)
                sb(ring, "rest_of_homes", [P, 3 * (UP + DOWN) - GROUPS * CHUNK])
                router = ExitStack()
                with router:
                    xn = sb(router, "xn", [P, TILES, D])
                    xnT = sb(router, "xnT", [P, 2, 2, KD, P])
                    logitsT = sb(router, "logitsT", [E, 4 * P])
                    logits = sb(router, "logits", [P, TILES, E])
                    top8 = sb(router, "top8", [P, TILES, 8])
                    struck = sb(router, "struck", [P, TILES, E])
                    chosen = sb(router, "chosen", [P, TILES // 2, 2, E])
                    expw = sb(router, "expw", [P, TILES, E])
                    wsum = sb(router, "wsum", [P, 2, TILES])
                    exp8 = sb(router, "exp8", [P, TILES, 8])
                    key_i32 = sb(router, "key_i32", [P, T // 2], i32)
                    key_of_column = sb(router, "key_of_column", [P, T // 2])
                    keys = sb(router, "keys", [P, T // 2])
                    best = sb(router, "best", [P, C])
                    merged = sb(router, "merged", [E, 2 * C])
                    slot_keys = sb(router, "slot_keys", [E, C])
                    pieces = [sb(router, f"piece{n}", [P, 2048]) for n in range(3)]
                experts = ExitStack()
                with experts:
                    slots = sb(experts, "slots", [P, 4, ROW])
                    slotsT = sb(experts, "slotsT", [P, 2, KD, P])
                    gate = sb(experts, "gate", [P, 2, F])
                    hidden = sb(experts, "hidden", [P, 2, F])
                    hiddenT = sb(experts, "hiddenT", [F, 2, P])
                    weight4 = sb(experts, "weight4", [P, 2, EG])
                    y_parts = sb(experts, "y_parts", [P, GROUPS, 2, D], f32r)
                    with ExitStack() as ring:
                        homes_e = homes(ring, "e", 3)
                    sumT = sb(experts, "sumT", [P, KD, T])
                    wo_piece = sb(experts, "wo_piece", [P, 2048])
                    sb(experts, "rest_of_homes_e", [P, 3 * (UP + DOWN) - KD * T - 2048])
        with ExitStack() as attention:
            xn4 = sb(attention, "xn4", [P, 4, D])
            xT = [sb(attention, f"xT_{n}", [P, KD, BT], f32r) for n in ("hi", "lo")]
            q = [sb(attention, f"q_{n}", [P, 2, G, BT], f32r) for n in ("hi", "lo")]
            k = [sb(attention, f"k_{n}", [P, 2, BT], f32r) for n in ("hi", "lo")]
            v = [sb(attention, f"v_{n}", [P, 4, KV * DH], f32r) for n in ("hi", "lo")]
            probs = sb(attention, "probs", [P, 2, 4, S])
            probsT = [sb(attention, f"probsT_{n}", [P, 2, 2, S], f32r) for n in ("hi", "lo")]
            o = [sb(attention, f"o_{n}", [P, 2, 2, S], f32r) for n in ("hi", "lo")]
            yT = sb(attention, "yT", [P, KD, BT])
            negmax = sb(attention, "negmax", [P, 2, 4])
            rowsum = sb(attention, "rowsum", [P, 2, 4])
            rowinv = sb(attention, "rowinv", [P, 2, 4])

        bank = [ctx.enter_context(nc.psum_tensor(f"bank{n}", [P, 512], f32)) for n in range(8)]
        sums_ps = [[bank[4], bank[6], bank[7], bank[3]], [bank[0], bank[1], bank[2], bank[5]]]
        scores_ps, probsT_ps, work_ps, out_ps = bank[0:2], bank[2:4], bank[4:6], bank[6:8]

        x_loaded = [sem(f"x_loaded{n}") for n in range(4)]
        small_loaded = sem("small_loaded")
        piece_loaded = [sem(f"piece_loaded{n}") for n in range(5)]
        weights_high = sem("weights_high")
        weights_split = sem("weights_split")
        bq_scaled = sem("bq_scaled")
        constants = sem("constants")
        key_raw = sem("key_raw")
        key_ready = sem("key_ready")
        setup_link = sem("setup_link")
        link = sem("dve_link")
        zero_stored = sem("zero_stored")
        xn_ready = sem("xn_ready")
        xnT_raw = sem("xnT_raw")
        xnT_ready = sem("xnT_ready")
        logitsT_raw = sem("logitsT_raw")
        logitsT_ready = sem("logitsT_ready")
        logits_raw = sem("logits_raw")
        logits_ready = sem("logits_ready")
        top8_ready = sem("top8_ready")
        shifted = sem("shifted")
        exps = sem("exps")
        chosen_ready = sem("chosen_ready")
        scaled_ready = sem("scaled_ready")
        shifted8 = sem("shifted8")
        winv_ready = sem("winv_ready")
        weights_ready = sem("weights_ready")
        chosenT_raw = sem("chosenT_raw")
        first_ready = sem("first_ready")
        slot_raw = sem("slot_raw")
        slot_ready = sem("slot_ready")
        table_written = sem("table_written")
        gathered = [sem(f"gathered{n}") for n in range(4)]
        slotsT_raw = sem("slotsT_raw")
        slotsT_ready = sem("slotsT_ready")
        up_done = sem("up_done")
        gate_ready = sem("gate_ready")
        hidden_ready = sem("hidden_ready")
        hiddenT_raw = sem("hiddenT_raw")
        hiddenT_ready = sem("hiddenT_ready")
        down_done = sem("down_done")
        weight_ready = sem("weight_ready")
        y_high = sem("y_high")
        down_free = sem("down_free")
        onehot_free = [sem(f"onehot_free{n}") for n in range(2)]
        onehot_ready = [sem(f"onehot_ready{n}") for n in range(2)]
        sum_free = [sem(f"sum_free{n}") for n in range(2)]
        sum_link = [sem(f"sum_link{n}") for n in range(2)]
        sumT_zeroed = sem("sumT_zeroed")
        sumT_ready = sem("sumT_ready")
        last_token_ready = sem("last_token_ready")
        last_token_raw = sem("last_token_raw")
        limit_ready = sem("limit_ready")
        sums_raw = sem("sums_raw")
        late_raw = [sem(f"late_raw{n}") for n in range(2)]
        late_final = [sem(f"late_final{n}") for n in range(2)]
        x_final = sem("x_final")
        out_stored = sem("out_stored")
        xn4_ready = sem("xn4_ready")
        work_ready = sem("work_ready")
        work_high = sem("work_high")
        work_taken = sem("work_taken")
        scores_ready = sem("scores_ready")
        negmax_ready = sem("negmax_ready")
        exp_ready = sem("exp_ready")
        probs_ready = sem("probs_ready")
        probsT_raw = sem("probsT_raw")
        probsT_high = sem("probsT_high")
        probsT_taken = sem("probsT_taken")
        y_raw = sem("y_raw")
        yT_ready = sem("yT_ready")
        y_ready = sem("y_ready")
        attention_done = sem("attention_done")

        layer_homes = [homes_r + homes_o + homes_e + homes_r + homes_o[:1] + homes_r,
                       homes_q + homes_r + homes_o + homes_e + homes_q[:3]]
        AHEAD = [len(homes_r + homes_o), len(homes_q + homes_r + homes_o)]
        last_of_e = [max(g for g in range(GROUPS) if layer_homes[layer][g] in homes_e) for layer in range(2)]

        def home(layer, g):
            return layer_homes[layer][g]

        def loads_before(layer, g):
            place = home(layer, g)[2]
            return sum(home(l, n)[2] is place for l in range(2) for n in range(GROUPS) if (l, n) <= (layer, g))

        def halves(t, n):
            return [w[:, n * H // 2:(n + 1) * H // 2, :] for w in t]
        splits = [(pieces[kd][:], wq_in[kd * P:kd * P + P, :], [(pieces[kd][:], *[w[:, kd, :] for w in wq])], SCALE) for kd in range(KD)]
        both = pieces[2][:].rearrange("p (w k n) -> p w k n", w=2, k=KD)
        splits.append((None, None, [(both[:, n], *[w[:] for w in t]) for n, t in enumerate((wk, wv))], 1.0))
        wide = wo_piece[:].rearrange("p (h d) -> p h d", d=D)
        for n in range(2):
            splits.append((wide, wo_in[n * T // 2:(n + 1) * T // 2, :].rearrange("(h p) d -> p h d", p=P),
                           [(wide, *halves(wo, n))], 1.0))

        def place(n):
            return n // 4 % KV, n % 4 // 2, n % 2

        first_fills = [("xT", 0, 0), ("xT", 1, 0), ("k", 0, 0), ("q", 0, 0), ("q", 1, 0), ("v", 0, 0),
                       ("v", 1, 0), ("q", 2, 0), ("q", 3, 0)]
        SCORES_AT = 6

        def fills(n, last):
            if last and n >= 12:
                return []
            kv = (n // 4 + 1) % KV
            r = n % 4
            more = [("k", 0, kv), ("q", 0, kv)] if r == 0 else [("q", r, kv)]
            if n == 11 and not last:
                more += [("xT", h, 0) for h in range(KD)]
            tile = {14: 0, 15: 1, 0: 2, 16: 2, 1: 3}.get(n)
            if tile is not None:
                more.append(("v", tile, 0))
            return more

        def each_chunk(engine, most, run):
            def two(pair):
                for n in range(2):
                    c = pair * 2 + n
                    with engine.If(most >= c * CHUNK):
                        run(c, bank[n])

            two(0)
            with engine.If(most >= 2 * CHUNK):
                with engine.Fori(1, CHUNKS // 2) as pair:
                    two(pair)

        block = ctx.enter_context(nc.Block())

        @block.sync
        def _(sp):
            for n in range(4):
                sp.dma_start(x[:, 4 * n:4 * n + 4, :],
                             x_in[512 * n:512 * n + 512, :].rearrange("(a p) d -> p a d", p=P)).then_inc(x_loaded[n], 16)
            for dst, src in ((router_w, router_in), (bq, bq_in), (bk, bk_in), (bv, bv_in), (bo, bo_in)):
                sp.dma_start(dst[:], src).then_inc(small_loaded, 16)

            for n in range(KD):
                sp.dma_start(splits[n][0], splits[n][1]).then_inc(piece_loaded[n], 16)
            for n, src in enumerate((wk_in, wv_in)):
                sp.dma_start(both[:, n], src.rearrange("(k p) n -> p k n", p=P)).then_inc(piece_loaded[2], 16)

            xn_seen, weights_seen, downs_seen = Tally(xn_ready), Tally(weights_ready), Tally(down_done)

            def load(layer, g):
                up_home, down_home, loaded = home(layer, g)
                sp.dma_start(up_home, up_in[g * P:g * P + P, :].rearrange("p (j k f) -> p j k f", j=EG, k=KD)).then_inc(loaded, 16)
                sp.dma_start(down_home, down_in[g * F:g * F + F, :].rearrange("f (j d) -> f j d", j=EG)).then_inc(loaded, 16)

            def expert_layer(layer):
                rows = table[0:T, :].rearrange("(h p b) e -> h p b e", h=2, p=P)
                for n in range(4):
                    sp.wait_ge(xn_ready, xn_seen.add(4))
                    for half in range(2):
                        sp.dma_start(rows[half, :, 2 * n:2 * n + 2, 0:D],
                                     xn[:, 4 * n + half:4 * n + half + 3:2, :]).then_inc(table_written, 16)
                sp.wait_ge(weights_ready, weights_seen.add())
                for half in range(2):
                    sp.dma_start(rows[half, :, :, D:ROW],
                                 expw[:, half:TILES:2, :]).then_inc(table_written, 16)
                sp.wait_ge(slot_ready, 2 * layer + 2)
                if layer == 0:
                    sp.wait_ge(weights_split, 4)
                sp.wait_ge(gathered[3], 16 * (GROUPS // 4 * layer + 1))
                groups, loads = ((5, 4), (2, 1))[layer]
                before = downs_seen.now()
                for g in range(AHEAD[layer], GROUPS):
                    earlier = [n for n in range(g) if home(layer, n) is home(layer, g)]
                    after = max([(g - AHEAD[layer]) * groups // loads] + [n + 1 for n in earlier])
                    if after:
                        sp.wait_ge(down_done, before + after)
                    if layer == 0 and g == GROUPS - 3:
                        assert earlier[-1] >= last_of_e[0]
                        sp.dma_start(splits[3][0], splits[3][1]).then_inc(piece_loaded[3], 16)
                    load(layer, g)
                downs_seen.add(GROUPS)

            for g in range(AHEAD[0]):
                load(0, g)
            expert_layer(0)
            sp.wait_ge(weights_split, 5)
            sp.dma_start(splits[4][0], splits[4][1]).then_inc(piece_loaded[4], 16)
            sp.wait_ge(work_ready, len(first_fills) + len(fills(0, False)) + 1 + (BLOCKS - 1) * (WORK_PER_BLOCK - 2)
                       + sum(len(fills(n, True)) + 1 for n in range(1, 11)) + len(fills(11, True)))
            for g in range(len(homes_q)):
                load(1, g)
            sp.wait_ge(attention_done, 1)
            for g in range(len(homes_q), AHEAD[1]):
                load(1, g)
            expert_layer(1)
            sp.wait_ge(limit_ready, 2)
            most = nc.sync.value_load(limit[0:1, 0:1], min_val=0, max_val=T)
            with nc.sync.If(most >= T // 2):
                sp.wait_ge(late_final[1], B // 2)
            result = out.rearrange("(b h p) d -> h p b d", h=2, p=P)
            sp.dma_start(result[1], x[:, 1:TILES:2, :]).then_inc(out_stored, 16)
            for m in range(B // 2):
                sp.wait_ge(x_final, B // 2 + m + 1)
                sp.dma_start(result[0, :, 2 * m:2 * m + 2, :], x[:, 4 * m:4 * m + 3:2, :]).then_inc(out_stored, 16)
            sp.wait_ge(out_stored, 16 * (1 + B // 2))

        @block.gpsimd
        def _(pool):
            nc.gpsimd.memset(ident[:], 0.0).then_inc(setup_link, 1)
            nc.gpsimd.iota(token_i32[:], pattern=[[1, CHUNK]], base=0, channel_multiplier=0).then_inc(setup_link, 1)
            nc.gpsimd.memset(zero_row[:], 0.0).then_inc(setup_link, 1)
            pool.wait_ge(setup_link, 3)
            nc.gpsimd.affine_select(out=ident[:], in_=ident[:], compare_op=ALU.not_equal, fill=1.0, base=0,
                                    pattern=[[-1, P]], channel_multiplier=1).then_inc(constants, 1)
            nc.gpsimd.tensor_copy(token_of_column[:], token_i32[:]).then_inc(constants, 1)
            pool.wait_ge(constants, 2)
            pool.dma_start(table[T:T + 1, :], zero_row[0:1, :]).then_inc(zero_stored, 16)

            raw, tops, exp_seen = Tally(key_raw), Tally(top8_ready), Tally(exps)
            scales = Tally(scaled_ready)
            masks, inv, slot_seen = Tally(chosen_ready), Tally(winv_ready), Tally(slot_ready)
            written = Tally(table_written)
            moved, weighed = Tally(slotsT_raw), Tally(weight_ready)

            def expert_layer(layer):
                for half in range(2):
                    nc.gpsimd.iota(key_i32[64 * half:64 * half + 64, :], pattern=[[-1, 4], [-1024, 2], [-8, P]],
                                    base=T - 4 * half, channel_multiplier=0).then_inc(key_raw, 1)
                    pool.wait_ge(key_raw, raw.add())
                nc.gpsimd.tensor_copy(key_of_column[:], key_i32[:]).then_inc(key_ready, 1)
                pool.wait_ge(top8_ready, tops.add(4))
                nc.gpsimd.tensor_tensor(expw[:], logits[:], top8[:, :, 0:1].to_broadcast([P, TILES, E]),
                                        ALU.subtract).then_inc(shifted, 1)
                pool.wait_ge(exps, exp_seen.add(2))
                pool.wait_ge(winv_ready, inv.add())
                nc.gpsimd.tensor_tensor(expw[:], expw[:], wsum[:, 1, :].unsqueeze(2).to_broadcast([P, TILES, E]),
                                        ALU.mult).then_inc(scaled_ready, 1)
                pool.wait_ge(chosen_ready, masks.add(4))
                pool.wait_ge(scaled_ready, scales.add())
                nc.gpsimd.tensor_tensor(
                    expw[:].rearrange("p (h i) e -> p h i e", h=2), expw[:].rearrange("p (h i) e -> p h i e", h=2),
                    chosen[:].rearrange("p i h e -> p h i e"), ALU.mult).then_inc(weights_ready, 1)
                pool.wait_ge(slot_ready, slot_seen.add(2))
                pool.wait_ge(table_written, written.add(160))
                pool.wait_ge(zero_stored, 16)
                for g in range(GROUPS):
                    if g >= 4:
                        pool.wait_ge(slotsT_raw, moved.add())
                        pool.wait_ge(weight_ready, weighed.add())
                    nc.gpsimd.indirect_dma_start(
                        out=slots[:, g % 4, :], out_offset=None, in_=table[:, :],
                        in_offset=bass.IndirectOffsetOnAxis(ap=slot_index[:, g:g + 1], axis=0),
                    ).then_inc(gathered[g % 4], 16)
                moved.add(4)
                weighed.add(4)
                pool.wait_ge(down_done, GROUPS * layer + last_of_e[layer] + 1)
                nc.gpsimd.memset(sumT[:], 0.0).then_inc(sumT_zeroed, 1)

            def split_low(n):
                for m, (whole, hi, lo) in enumerate(splits[n][2]):
                    pool.wait_ge(weights_high, sum(len(p[2]) for p in splits[:n]) + m + 1)
                    nc.gpsimd.tensor_tensor(lo, whole, hi.bitcast(f32), ALU.subtract).then_inc(weights_split, 1)

            expert_layer(0)
            for n in range(3, 5):
                split_low(n)
            pool.wait_ge(attention_done, 1)
            expert_layer(1)

        @block.scalar
        def _(act):
            xnT_seen, logits_seen, shift_seen = Tally(xnT_raw), Tally(logits_raw), Tally(shifted)
            logitsT_seen = Tally(logitsT_raw)
            sT_seen, up_seen, hT_seen, down_seen = Tally(slotsT_raw), Tally(up_done), Tally(hiddenT_raw), Tally(down_done)
            weight_seen = Tally(weight_ready)

            def slot_step(s, parity, nxt, cur, prev):
                if prev:
                    act.wait_ge(hiddenT_raw, hT_seen.add())
                    nc.scalar.copy(hiddenT[:, 1 - parity, :], bank[5 - parity][0:F, 0:P]).then_inc(hiddenT_ready, 1)
                if nxt:
                    act.wait_ge(slotsT_raw, sT_seen.add())
                    nc.scalar.copy(slotsT[:, 1 - parity, :, :].rearrange("p k t -> p (k t)"),
                                   bank[1 - parity][:, 0:KD * P]).then_inc(slotsT_ready, 1)
                if cur:
                    act.wait_ge(up_done, up_seen.add())
                    nc.scalar.activation(gate[:, parity, :], bank[2 + parity][:, 0:F], ACT.Silu).then_inc(gate_ready, 1)
                if prev:
                    act.wait_ge(weight_ready, weight_seen.add())
                    act.wait_ge(down_done, down_seen.add())
                    nc.scalar.activation(y_parts[:, ds(s - 1, 1), 0, :].rearrange("p a d -> p (a d)"), bank[7 - parity][:, 0:D],
                                         ACT.Identity, scale=slot_weight[:, ds(s - 1, 1)]).then_inc(y_high, 1)

            def warm(function):
                nc.scalar.activation(warmed[:], bo[:, 0:1], function)

            def expert_layer(layer):
                if layer == 0:
                    warm(ACT.Exp)
                def copies(i, parity, before=True):
                    for pair in range(2):
                        act.wait_ge(xnT_raw, xnT_seen.add())
                        nc.scalar.copy(xnT[:, pair].rearrange("p t k c -> p (t k c)"), bank[pair][:]).then_inc(xnT_ready, 1)
                    if before:
                        copy_logits(i - 1)
                    act.wait_ge(logitsT_raw, logitsT_seen.add())
                    nc.scalar.copy(logitsT[:], bank[3 + parity][0:E, :]).then_inc(logitsT_ready, 1)

                def copy_logits(i):
                    act.wait_ge(logits_raw, logits_seen.add())
                    nc.scalar.copy(logits[:, 4 * i:4 * i + 4, :].rearrange("p t e -> p (t e)"),
                                   bank[2][:, 0:4 * E]).then_inc(logits_ready, 1)

                for i in range(4):
                    copies(i, i % 2, i > 0)
                copy_logits(3)
                if layer == 0:
                    split_high(2)
                act.wait_ge(shifted8, layer + 1)
                nc.scalar.activation(exp8[:], exp8[:], ACT.Exp).then_inc(exps, 1)
                act.wait_ge(shifted, shift_seen.add())
                nc.scalar.activation(expw[:], expw[:], ACT.Exp).then_inc(exps, 1)
                warm(ACT.Silu)
                act.wait_ge(slotsT_raw, sT_seen.add())
                nc.scalar.copy(slotsT[:, 0, :, :].rearrange("p k t -> p (k t)"), bank[0][:, 0:KD * P]).then_inc(slotsT_ready, 1)
                slot_step(0, 0, True, True, False)
                with turns(nc.scalar, 3, [(hT_seen, 4), (sT_seen, 4), (up_seen, 4), (weight_seen, 4), (down_seen, 4)]) as i:
                    for u in range(4):
                        slot_step(i * 4 + 1 + u, (1 + u) % 2, True, True, True)
                for s in range(13, GROUPS + 1):
                    slot_step(s, s % 2, s < GROUPS - 1, s < GROUPS, True)
                if layer == 0:
                    split_high(3)
                act.wait_ge(limit_ready, layer + 1)
                act.wait_ge(sumT_zeroed, layer + 1)
                most = nc.scalar.value_load(limit[0:1, 0:1], min_val=0, max_val=T)

                def keep(c, sums):
                    act.wait_ge(onehot_free[layer], c * PARTS + 2 * PARTS)
                    nc.scalar.copy(sumT[:, :, c * CHUNK:c * CHUNK + CHUNK] if isinstance(c, int) else
                                   sumT[:, :, ds(c * CHUNK, CHUNK)],
                                   sums[:].rearrange("p (k t) -> p k t", k=KD)).then_inc(sum_free[layer], 1)

                each_chunk(nc.scalar, most, keep)
                nc.scalar.drain().then_inc(sumT_ready, 1)

            def split_high(n):
                act.wait_ge(piece_loaded[n], 16 * (2 if splits[n][0] is None else 1))
                for whole, hi, _ in splits[n][2]:
                    nc.scalar.activation(hi, whole, ACT.Copy, scale=splits[n][3]).then_inc(weights_high, 1)

            for n in range(2):
                split_high(n)
            act.wait_ge(small_loaded, 80)
            expert_layer(0)

            work_seen, pT_seen = Tally(work_ready), Tally(probsT_raw)
            scores_seen, max_seen, y_seen = Tally(scores_ready), Tally(negmax_ready), Tally(y_raw)
            uses = [0]

            def take_high(dst, bias=None):
                act.wait_ge(work_ready, work_seen.add())
                src = work_ps[uses[0] % 2]
                uses[0] += 1
                src = src[:] if dst.ndim == 2 else src[:].rearrange("p (h s) -> p h s", h=2)
                if bias is None:
                    nc.scalar.copy(dst, src).then_inc(work_high, 1)
                else:
                    nc.scalar.activation(dst, src, ACT.Identity, bias=bias).then_inc(work_high, 1)

            def take_fill(what, n, kv):
                if what == "k":
                    take_high(k[0][:, kv % 2, :], bk[:, kv:kv + 1])
                elif what == "q":
                    take_high(q[0][:, kv % 2, n, :], bq[:, G * kv + n:G * kv + n + 1])
                else:
                    take_high((xT if what == "xT" else v)[0][:, n, :])

            def exps_of(n, head):
                act.wait_ge(scores_ready, scores_seen.add())
                act.wait_ge(negmax_ready, max_seen.add())
                for qt in range(2):
                    t = 2 * head + qt
                    nc.scalar.activation(probs[:, n % 2, t, :], scores_ps[head][:, qt * S:qt * S + S], ACT.Exp,
                                         bias=negmax[:, n % 2, t:t + 1],
                                         accum_out=rowsum[:, n % 2, t:t + 1]).then_inc(exp_ready, 1)

            def output():
                act.wait_ge(y_raw, y_seen.add())
                for d in range(KD):
                    nc.scalar.activation(yT[:, d, :], out_ps[d][:], ACT.Identity, bias=bo[:, d:d + 1]).then_inc(yT_ready, 1)

            def step(n, last=False):
                kv, bb, hp = place(n)
                for head in range(2):
                    act.wait_ge(probsT_raw, pT_seen.add())
                    nc.scalar.copy(probsT[0][:, head].rearrange("p c s -> p (c s)"),
                                   probsT_ps[head][:]).then_inc(probsT_high, 1)
                jobs = fills(n, last)
                for head in range(2):
                    if not (last and n == 15):
                        exps_of(n + 1, head)
                    if head == 0 and jobs:
                        take_fill(*jobs.pop(0))
                for job in jobs:
                    take_fill(*job)
                if n == STEPS:
                    output()
                take_high(o[0][:, n % 2, :, :], bv[:, kv:kv + 1])
                if n == STEPS:
                    uses[0] += 2

            split_high(4)
            act.wait_ge(small_loaded, 80)
            act.wait_ge(bq_scaled, 1)
            warm(ACT.Exp)
            for n, job in enumerate(first_fills):
                take_fill(*job)
                if n >= SCORES_AT and n < SCORES_AT + 2:
                    exps_of(0, n - SCORES_AT)
            step(0)
            with turns(nc.scalar, BLOCKS - 1, [(work_seen, WORK_PER_BLOCK - 2), (pT_seen, 32), (scores_seen, 32),
                                               (max_seen, 32), (y_seen, 1)]):
                for n in range(1, STEPS + 1):
                    step(n)
            for n in range(1, STEPS):
                step(n, last=True)
            output()
            expert_layer(1)

        @block.vector
        def _(dve):
            linked = Tally(link)

            def tie(ins):
                ins.then_inc(link, 1)
                dve.wait_ge(link, linked.add())

            nc.vector.sem_inc(down_free, 2)
            tie(nc.vector.memset(quadrant[:], 0.0))
            for j in range(EG):
                last = nc.vector.memset(quadrant[32 * j:32 * j + 32, j:j + 1], 1.0)
            tie(last)
            logits_seen, key_seen, pairs_seen = Tally(logits_ready), Tally(key_ready), Tally(chosenT_raw)
            slot_seen, gates_seen = Tally(slot_raw), Tally(gate_ready)
            high_seen, sums_seen = Tally(y_high), Tally(sums_raw)
            for layer in range(2):
                nc.vector.sem_inc(onehot_free[layer], PARTS)
                nc.vector.sem_inc(sum_free[layer], 2)
                nc.vector.sem_inc(sum_link[layer], 1)
            arrived = [Tally(s) for s in gathered]

            def spread(tiles):
                for a in tiles:
                    last = nc.vector.bn_stats(stats[:, a, :], x[:, a, :])
                return last

            def moment_steps(a, b):
                even, odd = stats[:, a:b, 1], stats[:, a:b, 4]
                mean_, rstd_, half_gap, gap2, var = (ln[:, n, a:b] for n in range(5))

                def after_last(op, *args):
                    dve.wait_ge(link, linked.now())
                    op(*args).then_inc(link, 1)
                    linked.add()

                tt, ts, stt = nc.vector.tensor_tensor, nc.vector.tensor_scalar, nc.vector.scalar_tensor_tensor
                steps = [(tt, mean_, even, odd, ALU.add),
                         (tt, var, stats[:, a:b, 2], stats[:, a:b, 5], ALU.add),
                         (tt, half_gap, even, odd, ALU.subtract),
                         (stt, gap2, half_gap, 0.25, half_gap, ALU.mult, ALU.mult),
                         (ts, mean_, mean_, 0.5, None, ALU.mult),
                         (stt, var, var, 1.0 / D, gap2, ALU.mult, ALU.add),
                         (ts, var, var, EPS, None, ALU.add),
                         (ts, rstd_.bitcast(i32), var.bitcast(i32), -0.5, ROOT_BITS, ALU.mult, ALU.add)]
                steps += [(tt, gap2, rstd_, rstd_, ALU.mult),
                          (stt, gap2, gap2, -0.5, var, ALU.mult, ALU.mult),
                          (stt, rstd_, gap2, 1.5, rstd_, ALU.add, ALU.mult)] * 3
                return [lambda step=step: after_last(*step) for step in steps]

            def moments(a, b):
                for step in moment_steps(a, b):
                    step()
                dve.wait_ge(link, linked.now())

            def normalise(a, b):
                for a in range(a, b):
                    nc.vector.tensor_scalar(xn[:, a, :], x[:, a, :], mean[:, a:a + 1], rstd[:, a:a + 1],
                                            ALU.subtract, ALU.mult).then_inc(xn_ready, 1)

            def slot_step(s, parity, u, cur, prev):
                if cur:
                    dve.wait_ge(gathered[u], arrived[u].add(16))
                    tie(nc.vector.tensor_tensor(weight4[:, parity, :], slots[:, u, ds(s + D, EG, step=GROUPS)],
                                                quadrant[:], ALU.mult))
                    nc.vector.tensor_reduce(slot_weight[:, ds(s, 1)], weight4[:, parity, :], AX.X, ALU.add).then_inc(weight_ready, 1)
                    dve.wait_ge(gate_ready, gates_seen.add())
                    nc.vector.tensor_tensor(hidden[:, parity, :], gate[:, parity, :], bank[2 + parity][:, F:2 * F],
                                            ALU.mult).then_inc(hidden_ready, 1)
                if prev:
                    dve.wait_ge(y_high, high_seen.add())
                    nc.vector.scalar_tensor_tensor(
                        y_parts[:, ds(s - 1, 1), 1, :].rearrange("p a d -> p (a d)"), bank[7 - parity][:, 0:D],
                        slot_weight[:, ds(s - 1, 1)],
                        y_parts[:, ds(s - 1, 1), 0, :].rearrange("p a d -> p (a d)").bitcast(f32),
                        ALU.mult, ALU.subtract).then_inc(down_free, 1)

            def expert_layer(layer):
                for n in range(4):
                    dve.wait_ge(logits_ready, logits_seen.add())
                    for a in range(4 * n, 4 * n + 4):
                        last = nc.vector.max(top8[:, a, :], logits[:, a, :])
                    last.then_inc(top8_ready, 1)
                    dve.wait_ge(top8_ready, 4 * layer + n + 1)
                    if n == 3:
                        nc.vector.tensor_tensor(exp8[:], top8[:], top8[:, :, 0:1].to_broadcast([P, TILES, 8]),
                                                ALU.subtract).then_inc(shifted8, 1)
                    for a in range(4 * n, 4 * n + 4):
                        last = nc.vector.match_replace(struck[:, a, :], top8[:, a, :], logits[:, a, :], LOWEST)
                    tie(last)
                    nc.vector.tensor_scalar(chosen[:, n % 2 * 4:n % 2 * 4 + 4, n // 2, :], struck[:, 4 * n:4 * n + 4, :],
                                            0.99 * LOWEST, None, ALU.is_lt).then_inc(chosen_ready, 1)
                dve.wait_ge(key_ready, key_seen.add())
                for n in range(2):
                    dve.wait_ge(chosenT_raw, pairs_seen.add())
                    last = nc.vector.tensor_tensor(keys[:, 512 * n:512 * n + 512], bank[n][:],
                                                   key_of_column[:, 512 * n:512 * n + 512], ALU.mult)
                tie(last)
                for n in range(C // 8):
                    tie(nc.vector.max(best[:, 8 * n:8 * n + 8], keys[:]))
                    if n < C // 8 - 1:
                        tie(nc.vector.match_replace(keys[:], best[:, 8 * n:8 * n + 8], keys[:], -1.0))
                    if n == 0:
                        dve.wait_ge(exps, 2 * layer + 1)
                        tie(nc.vector.tensor_reduce(wsum[:, 0, :], exp8[:], AX.X, ALU.add))
                        tie(nc.vector.reciprocal(wsum[:, 1, :], wsum[:, 0, :]))
                        nc.vector.tensor_scalar(wsum[:, 1, :], wsum[:, 1, :], 0.5, None, ALU.mult).then_inc(winv_ready, 1)
                nc.vector.tensor_copy(merged[:, 0:C], best[0:E, :])
                tie(nc.vector.tensor_copy(merged[:, C:2 * C], best[E:P, :]))
                for n in range(C // 8):
                    last = nc.vector.max(first_keys(n), merged[:])
                    if n < C // 8 - 1:
                        tie(last)
                        tie(nc.vector.match_replace(merged[:], first_keys(n), merged[:], -1.0))
                last.then_inc(first_ready, 1)
                dve.wait_ge(slot_raw, slot_seen.add())
                for dst in (slot_token, slot_index):
                    nc.vector.tensor_scalar(dst[:], bank[4][:, 0:GROUPS], -1.0, float(T), ALU.mult, ALU.add).then_inc(slot_ready, 1)

                dve.wait_ge(slot_ready, 2 * layer + 2)
                tie(nc.vector.scalar_tensor_tensor(held_token[:], slot_token[:], float(T), slot_token[:], ALU.is_lt, ALU.mult))
                nc.vector.tensor_reduce(last_token[:, 0:1], held_token[:], AX.X, ALU.max).then_inc(last_token_ready, 1)
                if layer == 0:
                    split_low(2)
                slot_step(0, 0, 0, True, False)
                dve.wait_ge(last_token_raw, layer + 1)
                tie(nc.vector.reduce_max(last_token[0:1, 1:2], bank[5][0:1, 0:P], AX.X))
                nc.vector.tensor_copy(limit[:], last_token[0:1, 1:2]).then_inc(limit_ready, 1)
                with turns(nc.vector, 3, [(linked, 4), (gates_seen, 4), (high_seen, 4)] + [(t, 16) for t in arrived]) as i:
                    for u in range(4):
                        slot_step(i * 4 + 1 + u, (1 + u) % 2, (1 + u) % 4, True, True)
                for s in range(13, GROUPS + 1):
                    slot_step(s, s % 2, s % 4, s < GROUPS, True)

                dve.wait_ge(limit_ready, layer + 1)
                most = nc.vector.value_load(limit[0:1, 0:1], min_val=0, max_val=T)

                def mark(c, _):
                    dve.wait_ge(sum_link[layer], c + 1)
                    for part in range(PARTS):
                        dve.wait_ge(onehot_free[layer], c * PARTS + part + 1)
                        nc.vector.tensor_tensor(
                            onehot[:, part, :, :], token_of_column[:].unsqueeze(1).to_broadcast([P, PG, CHUNK]),
                            slot_token[:, PG * part:PG * part + PG].unsqueeze(2).to_broadcast([P, PG, CHUNK]),
                            ALU.is_equal).then_inc(onehot_ready[layer], 1)
                    dve.wait_ge(onehot_ready[layer], c * PARTS + PARTS)
                    nc.vector.tensor_scalar(slot_token[:], slot_token[:], -float(CHUNK), None,
                                            ALU.add).then_inc(sum_link[layer], 1)

                each_chunk(nc.vector, most, mark)
                with nc.vector.If(most >= T // 2):
                    for m in range(B // 2):
                        dve.wait_ge(late_raw[layer], m + 1)
                        add_sums(1, m).then_inc(late_final[layer], 1)
                    dve.wait_ge(late_final[layer], B // 2)
                    nc.vector.memset(held_token[:], 0.0)

            def add_sums(half, m):
                xa = x[:, 4 * m + half:4 * m + half + 3:2, :]
                return nc.vector.tensor_tensor(xa, xa, sums_ps[half][m][:].rearrange("p (a d) -> p a d", a=2), ALU.add)

            def add_early(m):
                dve.wait_ge(sums_raw, sums_seen.add())
                add_sums(0, m).then_inc(x_final, 1)

            def split_low(n):
                dve.wait_ge(weights_high, sum(len(p[2]) for p in splits[:n + 1]))
                for whole, hi, lo in splits[n][2]:
                    nc.vector.scalar_tensor_tensor(lo, whole, splits[n][3], hi.bitcast(f32), ALU.mult,
                                                   ALU.subtract).then_inc(weights_split, 1)

            def first_keys(n):
                return slot_keys[:, 8 * n:8 * n + 8]

            for n in range(2):
                for m in range(2):
                    dve.wait_ge(x_loaded[2 * n + m], 16)
                    last = spread(range(8 * n + 4 * m, 8 * n + 4 * m + 4))
                tie(last)
                moments(8 * n, 8 * n + 8)
                normalise(8 * n, 8 * n + 8)
            for n in range(KD):
                split_low(n)
            expert_layer(0)
            spread(range(1, TILES, 2))
            add_early(0)
            dve.wait_ge(x_final, 1)
            tie(spread((0, 2)))
            moments(0, 4)
            between = [lambda m=m: add_early(m) for m in range(1, 4)]
            between.append(lambda: dve.wait_ge(x_final, 4))
            between += [lambda a=a: spread((a, a + 2)) for a in (4, 8)]
            between.append(lambda: tie(spread((12, 14))))
            between += moment_steps(4, TILES)
            dve.wait_ge(small_loaded, 80)
            nc.vector.tensor_scalar(bq[:], bq[:], SCALE, None, ALU.mult).then_inc(bq_scaled, 1)
            dve.wait_ge(bq_scaled, 1)

            high_work, pT_high = Tally(work_high), Tally(probsT_high)
            scores_seen, exp_seen, y_seen = Tally(scores_ready), Tally(exp_ready), Tally(y_ready)
            uses, taken = [0], Tally(work_taken)

            def normalise_tokens(i):
                for t in range(4):
                    a = i * 4 + t if isinstance(i, int) else i * 4 + (t + 4)
                    last = nc.vector.tensor_scalar(xn4[:, t, :], x[:, ds(a, 1), :].rearrange("p a d -> p (a d)"),
                                                   mean[:, ds(a, 1)], rstd[:, ds(a, 1)], ALU.subtract, ALU.mult)
                last.then_inc(xn4_ready, 1)

            def take_low(hi, lo, bias=None):
                dve.wait_ge(work_high, high_work.add())
                src = work_ps[uses[0] % 2]
                uses[0] += 1
                src = src[:] if hi.ndim == 2 else src[:].rearrange("p (h s) -> p h s", h=2)
                if bias is None:
                    nc.vector.tensor_tensor(lo, src, hi.bitcast(f32), ALU.subtract).then_inc(work_taken, 1)
                else:
                    nc.vector.scalar_tensor_tensor(lo, src, bias, hi.bitcast(f32), ALU.add, ALU.subtract).then_inc(work_taken, 1)
                taken.add()

            def take_fill(what, n, kv):
                if what == "k":
                    take_low(*[t[:, kv % 2, :] for t in k], bk[:, kv:kv + 1])
                elif what == "q":
                    take_low(*[t[:, kv % 2, n, :] for t in q], bq[:, G * kv + n:G * kv + n + 1])
                else:
                    take_low(*[t[:, n, :] for t in (xT if what == "xT" else v)])

            def maxima(n):
                for head in range(2):
                    dve.wait_ge(scores_ready, scores_seen.add())
                    nc.vector.reduce_max(negmax[:, n % 2, 2 * head:2 * head + 2],
                                         scores_ps[head][:].rearrange("p (t s) -> p t s", t=2), AX.X,
                                         negate=True).then_inc(negmax_ready, 1)

            def normalise_probs(n):
                dve.wait_ge(exp_ready, exp_seen.add(4))
                tie(nc.vector.reciprocal(rowinv[:, n % 2, :], rowsum[:, n % 2, :]))
                for t in range(4):
                    last = nc.vector.tensor_scalar(probs[:, n % 2, t, :], probs[:, n % 2, t, :],
                                                   rowinv[:, n % 2, t:t + 1], None, ALU.mult)
                last.then_inc(probs_ready, 1)

            def output(i):
                for pair in range(2):
                    dve.wait_ge(y_ready, y_seen.add())
                    xa = x[:, ds(i * 4 + 2 * pair, 2), :].rearrange("p t d -> p (t d)")
                    nc.vector.tensor_tensor(xa, xa, work_ps[uses[0] % 2][:], ALU.add).then_inc(work_taken, 1)
                    uses[0] += 1
                    taken.add()
                dve.wait_ge(work_taken, taken.now())
                nc.vector.memset(last_token[:, 0:1], 0.0)
                for t in range(4):
                    last = nc.vector.bn_stats(stats[:, ds(i * 4 + t, 1), :].rearrange("p a n -> p (a n)"),
                                              x[:, ds(i * 4 + t, 1), :].rearrange("p a d -> p (a d)"))
                return last

            def chores(count):
                while between and count:
                    between.pop(0)()
                    count -= 1

            def step(n, i=None, last=False):
                kv, bb, hp = place(n)
                if not (last and n == 15):
                    maxima(n + 1)
                chores(3)
                for head in range(2):
                    dve.wait_ge(probsT_high, pT_high.add())
                    nc.vector.tensor_tensor(probsT[1][:, head].rearrange("p c s -> p (c s)"), probsT_ps[head][:],
                                            probsT[0][:, head].rearrange("p c s -> p (c s)").bitcast(f32),
                                            ALU.subtract).then_inc(probsT_taken, 1)
                jobs = fills(n, last)
                chores(5)
                for _ in range(2 if len(jobs) == 3 else len(jobs[:1])):
                    take_fill(*jobs.pop(0))
                chores(3)
                if not (last and n == 15):
                    normalise_probs(n + 1)
                for job in jobs:
                    take_fill(*job)
                    chores(3)
                if n == 9 and not last:
                    normalise_tokens(i)
                take_low(*[t[:, n % 2, :, :] for t in o], bv[:, kv:kv + 1])
                if n == STEPS:
                    output(i)

            dve.wait_ge(weights_split, SPLITS - 2)
            normalise_tokens(0)
            for n, job in enumerate(first_fills):
                take_fill(*job)
                if n == SCORES_AT - 1:
                    maxima(0)
                if n == SCORES_AT + 1:
                    normalise_probs(0)
                if between:
                    between.pop(0)()
            step(0)
            while between:
                between.pop(0)()
            with turns(nc.vector, BLOCKS - 1, [(linked, 16), (high_work, WORK_PER_BLOCK - 2), (taken, WORK_PER_BLOCK), (pT_high, 32),
                                               (scores_seen, 32), (exp_seen, 64), (y_seen, 2)]) as i:
                for n in range(1, STEPS + 1):
                    step(n, i)
            for n in range(1, STEPS):
                step(n, last=True)
            moments(0, TILES - 4)
            last = output(BLOCKS - 1)
            nc.vector.sem_inc(attention_done, 1)
            tie(last)
            normalise(0, 8)
            moments(TILES - 4, TILES)
            normalise(8, TILES)
            expert_layer(1)
            for m in range(B // 2):
                add_early(m)

        @block.tensor
        def _(pe):
            mm = nc.tensor.matmul
            xn_seen, xnT_seen, logits_taken = Tally(xn_ready), Tally(xnT_ready), Tally(logits_ready)
            chosen_seen, keys_seen = Tally(chosen_ready), Tally(first_ready)
            arrived = [Tally(s) for s in gathered]
            sT_seen, hidden_seen, hT_seen = Tally(slotsT_ready), Tally(hidden_ready), Tally(hiddenT_ready)
            free_seen, logitsT_seen = Tally(down_free), Tally(logitsT_ready)

            def transpose_slots(s, parity, u):
                pe.wait_ge(gathered[u], arrived[u].add(16))
                for kd in range(KD):
                    last = nc.tensor.transpose(bank[parity][:, kd * P:kd * P + P],
                                               slots[:, u, kd * P:kd * P + P], ident[:])
                last.then_inc(slotsT_raw, 1)

            def slot_step(layer, s, parity, nxt, cur, prev):
                if prev:
                    pe.wait_ge(hidden_ready, hidden_seen.add())
                    nc.tensor.transpose(bank[5 - parity][0:F, 0:P], hidden[:, 1 - parity, :], ident[:]).then_inc(hiddenT_raw, 1)
                if nxt:
                    transpose_slots(s + 1, 1 - parity, (s + 1) % 4)
                if cur:
                    pe.wait_ge(slotsT_ready, sT_seen.add())
                    up_home, _, loaded = home(layer, s)
                    pe.wait_ge(loaded, 32 * loads_before(layer, s))
                    for kd in range(KD):
                        for j in range(EG):
                            last = mm(bank[2 + parity][32 * j:32 * j + 32, 0:2 * F], slotsT[:, parity, kd, 32 * j:32 * j + 32],
                                      up_home[:, j, kd, :], start=kd == 0, stop=kd == KD - 1, tile_position=(0, 32 * j))
                    last.then_inc(up_done, 1)
                if prev:
                    pe.wait_ge(hiddenT_ready, hT_seen.add())
                    down_home = home(layer, s - 1)[1]
                    pe.wait_ge(down_free, free_seen.add())
                    for j in range(EG):
                        last = mm(bank[7 - parity][32 * j:32 * j + 32, 0:D], hiddenT[:, 1 - parity, 32 * j:32 * j + 32],
                                  down_home[:, j, :], start=True, stop=True, tile_position=(0, 32 * j))
                    last.then_inc(down_done, 1)

            def expert_layer(layer):
                def logits_of(n):
                    pe.wait_ge(logitsT_ready, logitsT_seen.add())
                    if logits_taken.now() > 0:
                        pe.wait_ge(logits_ready, logits_taken.now())
                    for t in range(4):
                        last = nc.tensor.transpose(bank[2][:, t * E:t * E + E], logitsT[:, t * P:t * P + P], ident[0:E, 0:E])
                    last.then_inc(logits_raw, 1)
                    logits_taken.add()

                def transpose_tokens(u):
                    pe.wait_ge(xn_ready, xn_seen.add(2))
                    for t in range(2):
                        for kd in range(KD):
                            c = (2 * t + kd) * P
                            last = nc.tensor.transpose(bank[u % 2][:, c:c + P], xn[:, 2 * u + t, kd * P:kd * P + P], ident[:])
                    last.then_inc(xnT_raw, 1)

                transpose_tokens(0)
                for u in range(8):
                    if u < 7:
                        transpose_tokens(u + 1)
                    pe.wait_ge(xnT_ready, xnT_seen.add())
                    n, pair = u // 2, u % 2
                    for kd in range(KD):
                        last = mm(bank[3 + n % 2][0:E, pair * 2 * P:(pair + 1) * 2 * P], router_w[:, kd, :],
                                  xnT[:, pair, :, kd, :], start=kd == 0, stop=kd == KD - 1)
                    if pair == 1:
                        last.then_inc(logitsT_raw, 1)
                    elif n > 0:
                        logits_of(n - 1)
                logits_of(3)
                chosen_seen.add(2)
                for n in range(2):
                    pe.wait_ge(chosen_ready, chosen_seen.add())
                    for c in range(4):
                        last = nc.tensor.transpose(bank[n][:, c * P:c * P + P],
                                                   chosen[:, 4 * n + c, :, :].rearrange("p h e -> p (h e)"), ident[:])
                    last.then_inc(chosenT_raw, 1)
                pe.wait_ge(first_ready, keys_seen.add())
                for j in range(EG):
                    last = mm(bank[4][32 * j:32 * j + 32, 0:GROUPS], slot_keys[:], ident[0:E, GROUPS * j:GROUPS * j + GROUPS],
                              start=True, stop=True, tile_position=(0, 32 * j))
                last.then_inc(slot_raw, 1)
                transpose_slots(0, 0, 0)
                for s in range(GROUPS + 1):
                    slot_step(layer, s, s % 2, s < GROUPS - 1, s < GROUPS, s > 0)
                    if s == 0:
                        pe.wait_ge(last_token_ready, layer + 1)
                        nc.tensor.transpose(bank[5][0:1, 0:P], last_token[:, 0:1], ident[:]).then_inc(last_token_raw, 1)
                pe.wait_ge(down_free, free_seen.now() + 2)

                pe.wait_ge(limit_ready, layer + 1)
                most = nc.tensor.value_load(limit[0:1, 0:1], min_val=0, max_val=T)

                def sum_chunk(c, sums):
                    pe.wait_ge(sum_free[layer], c + 1)
                    for part in range(PARTS):
                        pe.wait_ge(onehot_ready[layer], c * PARTS + part + 1)
                        for g in range(PG):
                            for low in range(2):
                                for kd in range(KD):
                                    last = mm(sums[:, kd * CHUNK:kd * CHUNK + CHUNK],
                                              y_parts[:, PG * part + g, low, kd * P:kd * P + P], onehot[:, part, g, :],
                                              start=part == g == low == kd == 0,
                                              stop=low == 1 and PG * part + g == GROUPS - 1, skip_group_check=True)
                        last.then_inc(onehot_free[layer], 1)

                each_chunk(nc.tensor, most, sum_chunk)
                pe.wait_ge(sumT_ready, layer + 1)
                columns = sumT[:].rearrange("p k (h s b) -> p k h b s", h=2, b=B)

                def back(half, signal):
                    for m in range(B // 2):
                        for n in range(2):
                            for kd in range(KD):
                                c = n * D + kd * P
                                last = nc.tensor.transpose(sums_ps[half][m][:, c:c + P], columns[:, kd, half, 2 * m + n, :], ident[:])
                        last.then_inc(signal, 1)

                with nc.tensor.If(most >= T // 2):
                    back(1, late_raw[layer])
                back(0, sums_raw)

            pe.wait_ge(constants, 2)
            pe.wait_ge(small_loaded, 80)
            expert_layer(0)

            xn4_seen, pT_taken, probs_seen, yT_seen = Tally(xn4_ready), Tally(probsT_taken), Tally(probs_ready), Tally(yT_ready)
            exp_seen, scored, uses = Tally(exp_ready), [False], [0]
            issued = Tally(work_taken)
            last_use = {}

            def work(*needed):
                back = min([1] + [uses[0] - last_use[what] for what in needed])
                if issued.turn is not None or issued.fixed > back:
                    pe.wait_ge(work_taken, issued.now(back=back))
                issued.add()
                uses[0] += 1
                return work_ps[(uses[0] - 1) % 2]

            def three(dst, w, m, start, stop, shared=False):
                mm(dst, w[0], m[0], start=start, stop=False, skip_group_check=shared)
                mm(dst, w[0], m[1], start=False, stop=False, skip_group_check=shared)
                return mm(dst, w[1], m[0], start=False, stop=stop, skip_group_check=shared)

            def on_chip(what):
                pe.wait_ge(work_taken, issued.now(back=uses[0] - last_use[what]))

            def project(what, n, kv, *needed):
                ps = work(*needed)
                if what == "xT":
                    for t in range(4):
                        last = nc.tensor.transpose(ps[:, t * P:t * P + P], xn4[:, t, n * P:n * P + P], ident[:])
                elif what == "v":
                    for kd in range(KD):
                        last = three(ps[:], [a[:, kd, n * P:n * P + P] for a in xT], [a[:, kd, :] for a in wv], kd == 0, kd == KD - 1)
                else:
                    w, c = (wk, kv * DH) if what == "k" else (wq, (G * kv + n) * DH)
                    for kd in range(KD):
                        last = three(ps[:], [a[:, kd, c:c + DH] for a in w], [a[:, kd, :] for a in xT], kd == 0, kd == KD - 1)
                last.then_inc(work_ready, 1)
                last_use[(what, n) if what in "qv" else what] = uses[0]

            def scores(n):
                kv, bb, hp = place(n)
                if n % 4 < 2:
                    on_chip(("q", 2 * hp + 1))
                for head in range(2):
                    if scored[0]:
                        pe.wait_ge(exp_ready, exp_seen.add(2))
                    for qt in range(2):
                        c = bb * S + qt * P
                        last = three(scores_ps[head][:, qt * S:qt * S + S], [a[:, kv % 2, 2 * hp + head, c:c + P] for a in q],
                                     [a[:, kv % 2, bb * S:bb * S + S] for a in k], True, True)
                    last.then_inc(scores_ready, 1)
                scored[0] = True

            def transpose_probs(n):
                pe.wait_ge(probs_ready, probs_seen.add())
                for head in range(2):
                    for qt in range(2):
                        for c in range(2):
                            last = nc.tensor.transpose(probsT_ps[head][:, c * S + qt * P:c * S + qt * P + P],
                                                       probs[:, n % 2, 2 * head + qt, c * P:c * P + P], ident[:])
                    last.then_inc(probsT_raw, 1)

            def output_product(n):
                kv, bb, hp = place(n)
                on_chip("o")
                for d in range(KD):
                    for head in range(2):
                        last = three(out_ps[d][:, bb * S:bb * S + S], [a[:, G * kv + 2 * hp + head, d * P:d * P + P] for a in wo],
                                     [a[:, n % 2, head, :] for a in o], n % STEPS == 0 and head == 0, n % STEPS == STEPS - 1 and head == 1,
                                     shared=True)
                if n % STEPS == STEPS - 1:
                    last.then_inc(y_raw, 1)

            def output():
                pe.wait_ge(yT_ready, yT_seen.add(KD))
                for pair in range(2):
                    ps = work()
                    for t in range(2):
                        for d in range(KD):
                            c = (2 * pair + t) * P
                            last = nc.tensor.transpose(ps[:, t * D + d * P:t * D + d * P + P], yT[:, d, c:c + P], ident[:])
                    last.then_inc(y_ready, 1)

            def step(n, last=False):
                kv, bb, hp = place(n)
                if not (last and n == 15):
                    scores(n + 1)
                transpose_probs(n)
                if n == STEPS:
                    output_product(n - 1)
                jobs = fills(n, last)
                for m, job in enumerate(jobs):
                    if n == 11 and job[0] == "xT" and job[1] == 0:
                        pe.wait_ge(xn4_ready, xn4_seen.add())
                    project(*job, *(["xT"] if n == 12 and m == 0 else []))
                    if m == 0 and 0 < n < STEPS:
                        output_product(n - 1)
                if not jobs:
                    output_product(n - 1)
                pe.wait_ge(probsT_taken, pT_taken.add(2))
                ps = work(*([("v", 2 * bb + 1)] if n % STEPS in (0, 2) else []))
                for c in range(2):
                    product = three(ps[:].rearrange("p (h s) -> p h s", h=2), [a[:, 2 * bb + c, kv * DH:kv * DH + DH] for a in v],
                                    [a[:, :, c, :] for a in probsT], c == 0, c == 1)
                product.then_inc(work_ready, 1)
                last_use["o"] = uses[0]
                if n == STEPS:
                    output()

            pe.wait_ge(weights_split, SPLITS - 2)
            pe.wait_ge(xn4_ready, xn4_seen.add())
            for n, job in enumerate(first_fills):
                if n == SCORES_AT:
                    scores(0)
                project(*job, *(["xT"] if n == KD else []))
            pe.wait_ge(x_final, B // 2)
            pe.wait_ge(weights_split, SPLITS)
            step(0)
            with turns(nc.tensor, BLOCKS - 1, [(issued, WORK_PER_BLOCK), (xn4_seen, 1), (pT_taken, 32), (probs_seen, 16),
                                               (exp_seen, 64), (yT_seen, KD)]):
                for n in range(1, STEPS + 1):
                    step(n)
            for n in range(1, STEPS):
                step(n, last=True)
            output_product(STEPS - 1)
            output()
            expert_layer(1)


def kernel(L0_attn_x, L0_attn_Wq, L0_attn_bq, L0_attn_Wk, L0_attn_bk, L0_attn_Wv, L0_attn_bv, L0_attn_Wo, L0_attn_bo,
           L0_ffn_router_w, L0_ffn_w1, L0_ffn_v1, L0_ffn_w2):
    import concourse.bacc as bacc
    from concourse.bass_utils import run_bass_kernel_spmd

    def arr(a):
        return np.ascontiguousarray(a)

    up = np.concatenate([np.asarray(L0_ffn_w1), np.asarray(L0_ffn_v1)], axis=1)
    up = up.reshape(EG, GROUPS, 2 * F, KD, P).transpose(1, 4, 0, 3, 2).reshape(GROUPS * P, EG * KD * 2 * F)
    down = np.asarray(L0_ffn_w2).reshape(EG, GROUPS, F, D).transpose(1, 2, 0, 3).reshape(GROUPS * F, EG * D)
    arrays = {
        "x_in": arr(np.asarray(L0_attn_x).reshape(T, D)),
        "wq_in": arr(L0_attn_Wq), "bq_in": arr(np.asarray(L0_attn_bq).reshape(H, DH).T),
        "wk_in": arr(L0_attn_Wk), "bk_in": arr(np.asarray(L0_attn_bk).reshape(KV, DH).T),
        "wv_in": arr(L0_attn_Wv), "bv_in": arr(np.asarray(L0_attn_bv).reshape(KV, DH).T),
        "wo_in": arr(L0_attn_Wo), "bo_in": arr(np.asarray(L0_attn_bo).reshape(KD, P).T),
        "router_in": arr(np.asarray(L0_ffn_router_w).reshape(E, KD, P).transpose(2, 1, 0)),
        "up_in": arr(up), "down_in": arr(down),
    }
    nc = bacc.Bacc("TRN2", target_bir_lowering=False, num_devices=1)
    args = [nc.dram_tensor(n, a.shape, mybir.dt.from_np(a.dtype), kind="ExternalInput").ap() for n, a in arrays.items()]
    result = nc.dram_tensor("out", (T, D), mybir.dt.float32, kind="ExternalOutput").ap()
    macaron_kernel(nc, *args, result)
    r = run_bass_kernel_spmd(nc, [arrays], core_ids=[0])
    return r.results[0]["out"].reshape(B, S, D)
```
